# Optimizing a Trainium2 kernel written in Bass

```python
import numpy as np
import jax
import jax.numpy as jnp

def _softmax(x, axis=-1):
    return jax.nn.softmax(x, axis=axis)

def _gelu(x):
    return jax.nn.gelu(x, approximate=True)

def _silu(x):
    return jax.nn.silu(x)

def _sigmoid(x):
    return jax.nn.sigmoid(x)

def _layernorm(x, axis=-1, eps=1e-05):
    m = jnp.mean(x, axis=axis, keepdims=True)
    v = jnp.var(x, axis=axis, keepdims=True)
    return (x - m) / jnp.sqrt(v + eps)

def _scatter_add(tgt, idx, src, axis=0):
    return tgt.at[idx].add(src)

def _segment_sum(src, seg, n):
    return jax.ops.segment_sum(src, seg, n)
kernel_name = 'mk_xattn_ffn_d1_seqx_r8_9951dc'

def setup_inputs(seed: int=0):
    np.random.seed(seed)
    _w = jnp.asarray

    def _rec_inputs():
        import jax
        import jax.numpy as jnp
        _rk = jax.random.key(seed)
        x = -0.000125 + 0.9999 * jax.random.normal(jax.random.fold_in(_rk, 1), (32, 64, 128), jnp.float32)
        _lenS = 64 - jax.random.randint(jax.random.fold_in(_rk, 7), (32,), 0, max(1, 64 // 4) + 1, jnp.int32)
        _lenS2 = 64 - jax.random.randint(jax.random.fold_in(_rk, 8), (32,), 0, max(1, 64 // 4) + 1, jnp.int32)
        _ctx_1024P = jax.random.normal(jax.random.fold_in(_rk, 11), (32, 16, 128), jnp.float32)
        _ctx_1024c = jax.random.dirichlet(jax.random.fold_in(_rk, 511), 0.3 * jnp.ones((16,), jnp.float32), (32, 64))
        _ctx_1024t = jnp.einsum('bsk,bkd->bsd', _ctx_1024c, _ctx_1024P)
        _ctx_1024t = _ctx_1024t * jax.lax.rsqrt(jnp.mean(jnp.square(_ctx_1024t)) + 1e-12) * 0.953939
        ctx_1024 = -1.52775e-05 + 0.999936 * (_ctx_1024t + 0.3 * jax.random.normal(jax.random.fold_in(_rk, 611), (32, 64, 128), jnp.float32))
        return (x, ctx_1024)
    x, ctx_1024 = _rec_inputs()

    def _L0_xattn_setup():
        import jax, jax.numpy as jnp
        import numpy as np
        D_MODEL = 128
        HEAD_SIZE = 128
        CONTEXT_SIZE = 128
        key = jax.random.key(seed)
        kq, kk, kv, kwq, kwk, kwv = jax.random.split(key, 6)
        B, S = (32, 128)
        scale = 1.0 / np.sqrt(D_MODEL)
        return {'query': jax.random.normal(kq, (B, S, D_MODEL), dtype=jnp.float32), 'key': jax.random.normal(kk, (B, S, D_MODEL), dtype=jnp.float32), 'value': jax.random.normal(kv, (B, S, D_MODEL), dtype=jnp.float32), 'w_q': jax.random.normal(kwq, (D_MODEL, HEAD_SIZE), dtype=jnp.float32) * scale, 'w_k': jax.random.normal(kwk, (D_MODEL, HEAD_SIZE), dtype=jnp.float32) * scale, 'w_v': jax.random.normal(kwv, (D_MODEL, HEAD_SIZE), dtype=jnp.float32) * scale, 'mask': 1}
    _L0_xattn_all = _L0_xattn_setup()
    _L0_xattn_in = {k: v for k, v in _L0_xattn_all.items() if k in ('w_q', 'w_k', 'w_v')}
    del _L0_xattn_all

    def _L0_ffn_setup():
        import jax, jax.numpy as jnp
        import numpy as np
        D_MODEL = 128
        N_EXPERTS = 8
        TOP_K = 2
        HIDDEN = 4 * D_MODEL
        key = jax.random.key(seed)
        ks = jax.random.split(key, 6)
        B, S = (2, 256)
        x = jax.random.normal(ks[0], (B, S, D_MODEL), dtype=jnp.float32)
        shared_w1 = jax.random.normal(ks[1], (HIDDEN, D_MODEL), dtype=jnp.float32) * 0.02
        shared_w2 = jax.random.normal(ks[2], (D_MODEL, HIDDEN), dtype=jnp.float32) * 0.02
        experts_w1 = jax.random.normal(ks[3], (N_EXPERTS, HIDDEN, D_MODEL), dtype=jnp.float32) * 0.02
        experts_w2 = jax.random.normal(ks[4], (N_EXPERTS, D_MODEL, HIDDEN), dtype=jnp.float32) * 0.02
        gate_w = jax.random.normal(ks[5], (N_EXPERTS, D_MODEL), dtype=jnp.float32) * 0.02
        return {'x': x, 'shared_w1': shared_w1, 'shared_w2': shared_w2, 'experts_w1': experts_w1, 'experts_w2': experts_w2, 'gate_w': gate_w}
    _L0_ffn_all = _L0_ffn_setup()
    _L0_ffn_in = {k: v for k, v in _L0_ffn_all.items() if k in ('shared_w1', 'shared_w2', 'experts_w1', 'experts_w2', 'gate_w')}
    del _L0_ffn_all
    return {'x': x, 'ctx_1024': ctx_1024, 'L0_xattn_w_q': _L0_xattn_in['w_q'], 'L0_xattn_w_k': _L0_xattn_in['w_k'], 'L0_xattn_w_v': _L0_xattn_in['w_v'], 'L0_ffn_shared_w1': _L0_ffn_in['shared_w1'], 'L0_ffn_shared_w2': _L0_ffn_in['shared_w2'], 'L0_ffn_experts_w1': _L0_ffn_in['experts_w1'], 'L0_ffn_experts_w2': _L0_ffn_in['experts_w2'], 'L0_ffn_gate_w': _L0_ffn_in['gate_w']}

def reference(x, ctx_1024, L0_xattn_w_q, L0_xattn_w_k, L0_xattn_w_v, L0_ffn_shared_w1, L0_ffn_shared_w2, L0_ffn_experts_w1, L0_ffn_experts_w2, L0_ffn_gate_w):
    import jax
    import jax.numpy as jnp

    def _L0_xattn_ref(query, key, value, w_q, w_k, w_v, mask):
        import jax, jax.numpy as jnp
        import numpy as np
        D_MODEL = 128
        HEAD_SIZE = 128
        CONTEXT_SIZE = 128
        q = jnp.einsum('bsd,dh->bsh', query, w_q)
        k = jnp.einsum('bsd,dh->bsh', key, w_k)
        v = jnp.einsum('bsd,dh->bsh', value, w_v)
        scale = 1.0 / np.sqrt(query.shape[-1]).astype(np.float32)
        scores = jnp.einsum('bqh,bkh->bqk', q, k) * scale
        if mask:
            S = scores.shape[1]
            causal = jnp.tril(jnp.ones((S, S), dtype=bool))
            scores = jnp.where(causal, scores, -jnp.inf)
        attn = jax.nn.softmax(scores, axis=-1)
        out = jnp.einsum('bqk,bkh->bqh', attn, v)
        return out

    def _L0_ffn_ref(x, shared_w1, shared_w2, experts_w1, experts_w2, gate_w):
        import jax, jax.numpy as jnp
        import numpy as np
        D_MODEL = 128
        N_EXPERTS = 8
        TOP_K = 2
        HIDDEN = 4 * D_MODEL
        B, S, D = x.shape
        T = B * S
        x_flat = x.reshape(T, D)
        shared = jnp.einsum('td,dh->th', x_flat, shared_w1.T)
        shared = jnp.einsum('th,hd->td', jax.nn.silu(shared), shared_w2.T)
        gate_logits = x_flat @ gate_w.T
        top_k_gates, top_k_idx = jax.lax.top_k(gate_logits, TOP_K)
        top_k_gates = jax.nn.softmax(top_k_gates, axis=1)
        gates = jnp.zeros((T, N_EXPERTS), dtype=x.dtype)
        gates = gates.at[jnp.arange(T)[:, None], top_k_idx].set(top_k_gates)
        h = jnp.einsum('td,ehd->teh', x_flat, experts_w1)
        expert_out = jnp.einsum('teh,edh->ted', jax.nn.silu(h), experts_w2)
        selected = jnp.einsum('ted,te->td', expert_out, gates)
        return (shared + selected).reshape(B, S, D)
    x = x + _L0_xattn_ref(_layernorm(x, axis=-1), ctx_1024, ctx_1024, L0_xattn_w_q, L0_xattn_w_k, L0_xattn_w_v, 1)
    x = x + _L0_ffn_ref(_layernorm(x, axis=-1), L0_ffn_shared_w1, L0_ffn_shared_w2, L0_ffn_experts_w1, L0_ffn_experts_w2, L0_ffn_gate_w)
    return x

_drawn_inputs = setup_inputs


def setup_inputs(seed=0):
    import zlib

    import numpy as np

    out = dict(_drawn_inputs(seed))
    spreads = {}
    factors = {}
    for name, (base, spread) in spreads.items():
        noise = np.random.default_rng([zlib.crc32(name.encode()), seed]).standard_normal(out[name].shape)
        drawn = base * np.exp(spread * noise) if base else spread * noise
        out[name] = jnp.asarray(drawn.astype(out[name].dtype))
    for name, factor in factors.items():
        out[name] = (out[name] * factor).astype(out[name].dtype)
    return out
```

```python
from contextlib import ExitStack

import concourse.bass as bass
from concourse import mybir

P = 128
F32 = mybir.dt.float32
I32 = mybir.dt.int32
ALU = mybir.AluOpType
ACT = mybir.ActivationFunctionType
AX_X = mybir.AxisListType.X

EPS = 1e-5
MASKED = -3.0e38
RSQRT_MAGIC = float(0x5F3759DF)


def build(nc, x_rows, x_cols, ctx_cols, wq_t, wk_t, w_v, gate_t, w1_cols, w2_cols, out_rows):
    _, TILES, D = x_rows.shape
    T = TILES * P
    NE = gate_t.shape[1]
    HID = w1_cols.shape[2]
    HC = HID // P
    S = 64
    GT = 4
    GROUPS = TILES // GT
    GW = GT * P
    SCALE = 1.0 / D ** 0.5

    with ExitStack() as ctx:
        def sb(name, shape, dt=F32):
            return ctx.enter_context(nc.sbuf_tensor(name, shape, dt))

        def bank(name, shape):
            return ctx.enter_context(nc.psum_tensor(name, shape, F32))

        def sem(name):
            return ctx.enter_context(nc.semaphore(name))

        x_sb = sb("x_sb", [P, TILES, D])
        xT_sb = sb("xT_sb", [P, T])
        cT_sb = sb("cT_sb", [P, T])
        wq_sb = sb("wq_sb", [P, D])
        wk_sb = sb("wk_sb", [P, D])
        wv_sb = sb("wv_sb", [P, D])
        gw_sb = sb("gw_sb", [P, NE])
        w1_sb = sb("w1_sb", [P, NE + 1, HID])
        w2_sb = sb("w2_sb", [P, NE + 1, HC, D])
        ident = sb("ident", [P, P])
        causal = sb("causal", [P, S])
        wq_c = sb("wq_c", [P, D])
        qk_w = sb("qk_w", [P, D])
        tT = sb("tT", [P, 2, GW])
        v_sb = sb("v_sb", [P, 2, GT, D + 1])
        s_sb = sb("s_sb", [P, GT, S])
        s_max = sb("s_max", [P, GT])
        probs = sb("probs", [P, 2, GT, P])
        pT = sb("pT", [P, GT, P])
        rsum = sb("rsum", [P, GT])
        stat1 = sb("stat1", [P, TILES, 6])
        mv1 = sb("mv1", [P, TILES, 2])
        rstd1 = sb("rstd1", [P, TILES])
        stat2 = sb("stat2", [P, TILES, 6])
        mv2 = sb("mv2", [P, TILES, 2])
        rstd2 = sb("rstd2", [P, TILES])
        ve = sb("ve", [P, TILES])
        newton = sb("newton", [P, TILES])
        x2 = sb("x2", [P, TILES, D])
        x2n = sb("x2n", [P, TILES, D])
        x2nT = sb("x2nT", [P, T])
        logits = sb("logits", [P, TILES, NE])
        rank_key = sb("rank_key", [P, TILES, NE])
        first = sb("first", [P, TILES, NE])
        second = sb("second", [P, TILES, NE])
        rest = sb("rest", [P, TILES, NE])
        tmp = sb("tmp", [P, TILES, NE])
        m1 = sb("m1", [P, TILES])
        m2 = sb("m2", [P, TILES])
        key = sb("key", [P, TILES])
        e2 = sb("e2", [P, TILES])
        g1 = sb("g1", [P, TILES])
        g2 = sb("g2", [P, TILES])
        gates = sb("gates", [P, TILES, NE])
        h_sb = sb("h_sb", [P, 2, HC, GW])
        out_sb = sb("out_sb", [P, TILES, D])

        banks = [bank(f"bank{i}", [P, 512]) for i in range(8)]
        ps_t, ps_v, ps_s, ps_pT, ps_o0, ps_o1, ps_x, ps_l = banks

        ld_w = sem("ld_w")
        ld_x = [sem(f"ld_x{i}") for i in range(GROUPS)]
        ld_xT = [sem(f"ld_xT{i}") for i in range(GROUPS)]
        ld_cT = [sem(f"ld_cT{i}") for i in range(GROUPS)]
        ld_ffn = [sem(f"ld_ffn{i}") for i in range(3)]
        consts_done = sem("consts_done")
        wq_centred = sem("wq_centred")
        qkw_psum = sem("qkw_psum")
        qkw_done = sem("qkw_done")
        t_psum = sem("t_psum")
        t_sbuf = sem("t_sbuf")
        v_psum = sem("v_psum")
        v_sbuf = sem("v_sbuf")
        s_psum = sem("s_psum")
        s_read = sem("s_read")
        s_ready = sem("s_ready")
        exp_done = sem("exp_done")
        pT_psum = sem("pT_psum")
        pT_sbuf = sem("pT_sbuf")
        o_psum = sem("o_psum")
        x2_done = sem("x2_done")
        x2n_done = sem("x2n_done")
        x2nT_psum = sem("x2nT_psum")
        x2nT_sbuf = sem("x2nT_sbuf")
        l_psum = sem("l_psum")
        e2_in = sem("e2_in")
        e2_done = sem("e2_done")
        h_psum = sem("h_psum")
        h_sbuf = sem("h_sbuf")
        y_psum = sem("y_psum")
        y_read = sem("y_read")
        stored = sem("stored")
        dve_step = sem("dve_step")
        pool_step = sem("pool_step")

        STEPS = (NE + 1) * GROUPS

        def expert_ld(e):
            return 0 if e == 0 else (1 if e <= 4 else 2)

        block = ctx.enter_context(nc.Block())

        @block.sync
        def _(sp):
            sp.dma_start(wq_sb[:], wq_t).then_inc(ld_w, 16)
            sp.dma_start(wk_sb[:], wk_t).then_inc(ld_w, 16)
            sp.dma_start(wv_sb[:], w_v).then_inc(ld_w, 16)
            sp.dma_start(gw_sb[:], gate_t).then_inc(ld_w, 16)
            for g in range(GROUPS):
                cols, tiles = slice(g * GW, (g + 1) * GW), slice(g * GT, (g + 1) * GT)
                sp.dma_start(xT_sb[:, cols], x_cols[:, cols]).then_inc(ld_xT[g], 16)
                sp.dma_start(cT_sb[:, cols], ctx_cols[:, cols]).then_inc(ld_cT[g], 16)
                sp.dma_start(x_sb[:, tiles, :], x_rows[:, tiles, :]).then_inc(ld_x[g], 16)
            for k, (a, b) in enumerate([(0, 1), (1, 5), (5, 9)]):
                sp.dma_start(w1_sb[:, a:b, :], w1_cols[:, a:b, :]).then_inc(ld_ffn[k], 16)
                sp.dma_start(w2_sb[:, a:b, :, :], w2_cols[:, a:b, :, :]).then_inc(ld_ffn[k], 16)
            for g in range(GROUPS):
                sp.wait_ge(y_read, NE * GROUPS + g + 1)
                tiles = slice(g * GT, (g + 1) * GT)
                sp.dma_start(out_rows[:, tiles, :], out_sb[:, tiles, :]).then_inc(stored, 16)
            sp.wait_ge(stored, 16 * GROUPS)

        @block.gpsimd
        def _(pool):
            nc.gpsimd.memset(ident[:], 0.0)
            nc.gpsimd.memset(causal[:], 0.0)
            nc.gpsimd.memset(v_sb[:, :, :, D:D + 1], 1.0)
            nc.gpsimd.iota(rank_key[:], pattern=[[0, TILES], [-1, NE]], base=NE, channel_multiplier=0,
                           allow_small_or_imprecise_dtypes=True).then_inc(pool_step, 1)
            pool.wait_ge(pool_step, 1)
            nc.gpsimd.affine_select(out=ident[:], in_=ident[:], compare_op=ALU.not_equal, fill=1.0, base=0,
                                    pattern=[[-1, P]], channel_multiplier=1).then_inc(pool_step, 1)
            for b in range(2):
                rows = slice(b * S, (b + 1) * S)
                pool.wait_ge(pool_step, 2 + b)
                last = nc.gpsimd.affine_select(out=causal[rows, :], in_=causal[rows, :], compare_op=ALU.is_ge,
                                               fill=MASKED, base=0, pattern=[[-1, S]], channel_multiplier=1)
                last.then_inc(pool_step, 1)
            pool.wait_ge(pool_step, 4)
            nc.gpsimd.memset(probs[:], 0.0).then_inc(consts_done, 1)

        @block.tensor
        def _(pe):
            pe.wait_ge(wq_centred, 1)
            nc.tensor.matmul(ps_x[:, 0:D], wq_c[:], wk_sb[:], start=True, stop=True).then_inc(qkw_psum, 1)
            pe.wait_ge(consts_done, 1)

            def project(g):
                pe.wait_ge(ld_xT[g], 16)
                if g == 0:
                    pe.wait_ge(qkw_done, 1)
                else:
                    pe.wait_ge(t_sbuf, g)
                nc.tensor.matmul(ps_t[:], qk_w[:], xT_sb[:, g * GW:(g + 1) * GW], start=True,
                                 stop=True).then_inc(t_psum, 1)
                pe.wait_ge(ld_cT[g], 16)
                if g:
                    pe.wait_ge(v_sbuf, g)
                for i in range(GT):
                    at = g * GW + i * P
                    last = nc.tensor.matmul(ps_v[:, i * D:(i + 1) * D], cT_sb[:, at:at + P], wv_sb[:],
                                            start=True, stop=True)
                last.then_inc(v_psum, 1)

            def score(g):
                pe.wait_ge(t_sbuf, g + 1)
                if g:
                    pe.wait_ge(s_read, g)
                for i in range(GT):
                    for b in range(2):
                        at = i * P + b * S
                        last = nc.tensor.matmul(ps_s[b * S:(b + 1) * S, i * S:(i + 1) * S],
                                                tT[:, g % 2, at:at + S],
                                                cT_sb[:, g * GW + at:g * GW + at + S], start=True, stop=True)
                last.then_inc(s_psum, 1)

            def attend(g):
                pe.wait_ge(exp_done, g + 1)
                if g:
                    pe.wait_ge(pT_sbuf, g)
                for i in range(GT):
                    last = nc.tensor.transpose(ps_pT[:, i * P:(i + 1) * P], probs[:, g % 2, i, :], ident[:])
                last.then_inc(pT_psum, 1)
                pe.wait_ge(pT_sbuf, g + 1)
                pe.wait_ge(v_sbuf, g + 1)
                if g:
                    pe.wait_ge(x2_done, g)
                for i in range(GT):
                    dst = (ps_o0, ps_o1)[i // 2]
                    at = (i % 2) * 256
                    last = nc.tensor.matmul(dst[:, at:at + D + 1], pT[:, i, :], v_sb[:, g % 2, i, :],
                                            start=True, stop=True)
                last.then_inc(o_psum, 1)

            def gate(g):
                pe.wait_ge(x2n_done, g + 1)
                if g:
                    pe.wait_ge(x2nT_sbuf, g)
                for i in range(GT):
                    last = nc.tensor.transpose(ps_x[:, i * P:(i + 1) * P], x2n[:, g * GT + i, :], ident[:])
                last.then_inc(x2nT_psum, 1)
                pe.wait_ge(x2nT_sbuf, g + 1)
                for i in range(GT):
                    t = g * GT + i
                    last = nc.tensor.matmul(ps_l[:, t * NE:(t + 1) * NE], x2nT[:, t * P:(t + 1) * P], gw_sb[:],
                                            start=True, stop=True)
                last.then_inc(l_psum, 1)

            project(0)
            for g in range(GROUPS):
                score(g)
                if g + 1 < GROUPS:
                    project(g + 1)
                if g:
                    gate(g - 1)
                attend(g)
            gate(GROUPS - 1)

            def up(n):
                e, g = divmod(n, GROUPS)
                pe.wait_ge(ld_ffn[expert_ld(e)], 32)
                for c in range(HC):
                    if n:
                        pe.wait_ge(h_sbuf, HC * (n - 1) + c + 1)
                    nc.tensor.matmul(banks[c][:], w1_sb[:, e, c * P:(c + 1) * P], x2nT[:, g * GW:(g + 1) * GW],
                                     start=True, stop=True).then_inc(h_psum, 1)

            def down(n):
                e, g = divmod(n, GROUPS)
                pe.wait_ge(h_sbuf, HC * (n + 1))
                if n >= 2:
                    pe.wait_ge(y_read, n - 1)
                if n == 1:
                    pe.wait_ge(x2_done, GROUPS)
                for i in range(GT):
                    for c in range(HC):
                        last = nc.tensor.matmul(banks[4 + n % 2][:, i * D:(i + 1) * D],
                                                h_sb[:, n % 2, c, i * P:(i + 1) * P], w2_sb[:, e, c, :],
                                                start=(c == 0), stop=(c == HC - 1))
                last.then_inc(y_psum, 1)

            up(0)
            for n in range(1, STEPS):
                up(n)
                down(n - 1)
            down(STEPS - 1)

        @block.scalar
        def _(act):
            act.wait_ge(qkw_psum, 1)
            nc.scalar.activation(qk_w[:], ps_x[:, 0:D], ACT.Copy, scale=SCALE).then_inc(qkw_done, 1)
            act.wait_ge(consts_done, 1)

            def evacuate_projections(g):
                act.wait_ge(t_psum, g + 1)
                if g >= 2:
                    act.wait_ge(s_psum, g - 1)
                nc.scalar.activation(tT[:, g % 2, :], ps_t[:], ACT.Copy).then_inc(t_sbuf, 1)
                act.wait_ge(v_psum, g + 1)
                if g >= 2:
                    act.wait_ge(o_psum, g - 1)
                nc.scalar.activation(v_sb[:, g % 2, :, 0:D], ps_v[:].rearrange("p (i d) -> p i d", i=GT),
                                     ACT.Copy).then_inc(v_sbuf, 1)

            def softmax_exp(g):
                act.wait_ge(s_ready, g + 1)
                if g >= 2:
                    act.wait_ge(pT_psum, g - 1)
                for b in range(2):
                    rows = slice(b * S, (b + 1) * S)
                    last = nc.scalar.activation(probs[rows, g % 2, :, b * S:(b + 1) * S], s_sb[rows, :, :], ACT.Exp)
                last.then_inc(exp_done, 1)

            def evacuate_pT(g):
                act.wait_ge(pT_psum, g + 1)
                if g:
                    act.wait_ge(o_psum, g)
                nc.scalar.activation(pT[:], ps_pT[:].rearrange("p (i q) -> p i q", i=GT),
                                     ACT.Copy).then_inc(pT_sbuf, 1)

            def evacuate_x2nT(g):
                act.wait_ge(x2nT_psum, g + 1)
                nc.scalar.activation(x2nT[:, g * GW:(g + 1) * GW], ps_x[:], ACT.Copy).then_inc(x2nT_sbuf, 1)

            evacuate_projections(0)
            for g in range(GROUPS):
                if g + 1 < GROUPS:
                    evacuate_projections(g + 1)
                if g:
                    evacuate_x2nT(g - 1)
                softmax_exp(g)
                evacuate_pT(g)
            evacuate_x2nT(GROUPS - 1)
            act.wait_ge(e2_in, 1)
            nc.scalar.activation(e2[:], m2[:], ACT.Exp).then_inc(e2_done, 1)
            for n in range(STEPS):
                for c in range(HC):
                    act.wait_ge(h_psum, HC * n + c + 1)
                    if n >= 2 and c == 0:
                        act.wait_ge(y_psum, n - 1)
                    nc.scalar.activation(h_sb[:, n % 2, c, :], banks[c][:], ACT.Silu).then_inc(h_sbuf, 1)

        @block.vector
        def _(dve):
            steps = [0]

            def link(ins):
                steps[0] += 1
                ins.then_inc(dve_step, 1)
                dve.wait_ge(dve_step, steps[0])

            V = nc.vector

            def rsqrt(dst, var, y, v):
                link(V.tensor_scalar(v, var, EPS, None, ALU.add))
                link(V.tensor_scalar(dst.bitcast(I32), v.bitcast(I32), 1, None, ALU.logical_shift_right))
                link(V.tensor_scalar(dst.bitcast(I32), dst.bitcast(I32), -1.0, RSQRT_MAGIC, ALU.mult, ALU.add))
                for _ in range(3):
                    link(V.tensor_tensor(y, v, dst, ALU.mult))
                    link(V.scalar_tensor_tensor(y, y, -0.5, dst, ALU.mult, ALU.mult))
                    link(V.scalar_tensor_tensor(dst, y, 1.5, dst, ALU.add, ALU.mult))

            def norm1(g):
                dve.wait_ge(ld_x[g], 16)
                tiles = slice(g * GT, (g + 1) * GT)
                for i in range(g * GT, (g + 1) * GT):
                    last = V.bn_stats(stat1[:, i, :], x_sb[:, i, :])
                link(last)
                for i in range(g * GT, (g + 1) * GT):
                    last = V.bn_aggr(mv1[:, i, :], stat1[:, i, :])
                link(last)
                rsqrt(rstd1[:, tiles], mv1[:, tiles, 1], newton[:, tiles], ve[:, tiles])

            def softmax(g):
                dve.wait_ge(s_psum, g + 1)
                if g:
                    dve.wait_ge(exp_done, g)
                for i in range(GT):
                    last = V.scalar_tensor_tensor(s_sb[:, i, :], ps_s[:, i * S:(i + 1) * S],
                                                  rstd1[:, g * GT + i:g * GT + i + 1], causal[:], ALU.mult, ALU.add)
                last.then_inc(s_read, 1)
                dve.wait_ge(s_read, g + 1)
                link(V.reduce_max(s_max[:], s_sb[:], AX_X))
                V.tensor_tensor(s_sb[:], s_sb[:], s_max[:].unsqueeze(2).to_broadcast([P, GT, S]),
                                ALU.subtract).then_inc(s_ready, 1)

            def residual(g):
                dve.wait_ge(o_psum, g + 1)
                for j, ps in enumerate((ps_o0, ps_o1)):
                    sums = ps[:].rearrange("p (i c) -> p i c", i=2)[:, :, D]
                    last = V.reciprocal(rsum[:, 2 * j:2 * j + 2], sums)
                link(last)
                for i in range(GT):
                    src = (ps_o0, ps_o1)[i // 2]
                    at = (i % 2) * 256
                    last = V.scalar_tensor_tensor(x2[:, g * GT + i, :], src[:, at:at + D], rsum[:, i:i + 1],
                                                  x_sb[:, g * GT + i, :], ALU.mult, ALU.add)
                last.then_inc(x2_done, 1)
                dve.wait_ge(x2_done, g + 1)

            def norm2(g):
                tiles = slice(g * GT, (g + 1) * GT)
                for i in range(g * GT, (g + 1) * GT):
                    last = V.bn_stats(stat2[:, i, :], x2[:, i, :])
                link(last)
                for i in range(g * GT, (g + 1) * GT):
                    last = V.bn_aggr(mv2[:, i, :], stat2[:, i, :])
                link(last)
                rsqrt(rstd2[:, tiles], mv2[:, tiles, 1], newton[:, tiles], ve[:, tiles])
                for i in range(g * GT, (g + 1) * GT):
                    last = V.tensor_scalar(x2n[:, i, :], x2[:, i, :], mv2[:, i, 0:1], rstd2[:, i:i + 1],
                                           ALU.subtract, ALU.mult)
                last.then_inc(x2n_done, 1)

            dve.wait_ge(ld_w, 64)
            link(V.bn_stats(stat1[:, 0, :], wq_sb[:]))
            link(V.bn_aggr(mv1[:, 0, :], stat1[:, 0, :]))
            V.tensor_scalar(wq_c[:], wq_sb[:], mv1[:, 0, 0:1], None, ALU.subtract).then_inc(wq_centred, 1)
            dve.wait_ge(wq_centred, 1)
            norm1(0)
            dve.wait_ge(consts_done, 1)
            for g in range(GROUPS):
                softmax(g)
                if g + 1 < GROUPS:
                    norm1(g + 1)
                residual(g)
                norm2(g)

            dve.wait_ge(l_psum, GROUPS)
            link(V.tensor_copy(logits[:], ps_l[:, 0:TILES * NE].rearrange("p (i e) -> p i e", e=NE)))

            def wide(a):
                return a.unsqueeze(2).to_broadcast([P, TILES, NE])

            def pick(one_hot, values, top):
                link(V.reduce_max(top[:], values[:], AX_X))
                link(V.tensor_tensor(tmp[:], values[:], wide(top[:]), ALU.is_equal))
                link(V.tensor_tensor(tmp[:], tmp[:], rank_key[:], ALU.mult))
                link(V.reduce_max(key[:], tmp[:], AX_X))
                link(V.tensor_tensor(one_hot[:], tmp[:], wide(key[:]), ALU.is_equal))

            pick(first, logits, m1)
            link(V.scalar_tensor_tensor(rest[:], first[:], MASKED, logits[:], ALU.mult, ALU.add))
            pick(second, rest, m2)
            V.tensor_tensor(m2[:], m2[:], m1[:], ALU.subtract).then_inc(e2_in, 1)
            dve.wait_ge(e2_done, 1)
            link(V.tensor_scalar(g1[:], e2[:], 1.0, None, ALU.add))
            link(V.reciprocal(g1[:], g1[:]))
            link(V.tensor_tensor(g2[:], e2[:], g1[:], ALU.mult))
            link(V.tensor_tensor(tmp[:], first[:], wide(g1[:]), ALU.mult))
            link(V.tensor_tensor(gates[:], second[:], wide(g2[:]), ALU.mult))
            link(V.tensor_tensor(gates[:], gates[:], tmp[:], ALU.add))
            for n in range(STEPS):
                e, g = divmod(n, GROUPS)
                dve.wait_ge(y_psum, n + 1)
                ps = banks[4 + n % 2]
                if e == 0:
                    V.tensor_tensor(out_sb[:, g * GT:(g + 1) * GT, :], ps[:].rearrange("p (i d) -> p i d", i=GT),
                                    x2[:, g * GT:(g + 1) * GT, :], ALU.add).then_inc(y_read, 1)
                    continue
                if g == 0:
                    dve.wait_ge(y_read, n)
                for i in range(GT):
                    t = g * GT + i
                    last = V.scalar_tensor_tensor(out_sb[:, t, :], ps[:, i * D:(i + 1) * D],
                                                  gates[:, t, e - 1:e], out_sb[:, t, :], ALU.mult, ALU.add)
                last.then_inc(y_read, 1)


_OUT_SHAPE = (128, 16, 128)


def kernel(x, ctx_1024, L0_xattn_w_q, L0_xattn_w_k, L0_xattn_w_v, L0_ffn_shared_w1, L0_ffn_shared_w2,
           L0_ffn_experts_w1, L0_ffn_experts_w2, L0_ffn_gate_w):
    import numpy as np
    import concourse.bacc as bacc
    from concourse.bass_utils import run_bass_kernel_spmd

    B, S, D = x.shape
    tiles = B * S // 128
    HID = L0_ffn_shared_w1.shape[0]
    w1 = np.concatenate([np.asarray(L0_ffn_shared_w1)[None], np.asarray(L0_ffn_experts_w1)])
    w2 = np.concatenate([np.asarray(L0_ffn_shared_w2)[None], np.asarray(L0_ffn_experts_w2)])
    laid_out = {
        "x_rows": np.asarray(x).reshape(tiles, 128, D).transpose(1, 0, 2),
        "x_cols": np.asarray(x).reshape(B * S, D).T,
        "ctx_cols": np.asarray(ctx_1024).reshape(B * S, D).T,
        "wq_t": np.asarray(L0_xattn_w_q).T,
        "wk_t": np.asarray(L0_xattn_w_k).T,
        "w_v": np.asarray(L0_xattn_w_v),
        "gate_t": np.asarray(L0_ffn_gate_w).T,
        "w1_cols": w1.transpose(2, 0, 1),
        "w2_cols": w2.transpose(2, 0, 1).reshape(HID // 128, 128, w2.shape[0], D).transpose(1, 2, 0, 3),
    }
    nc = bacc.Bacc("TRN2", target_bir_lowering=False, num_devices=1)
    arrays, args = {}, []
    for name, a in laid_out.items():
        arrays[name] = np.ascontiguousarray(a)
        args.append(nc.dram_tensor(name, a.shape, mybir.dt.from_np(a.dtype), kind="ExternalInput").ap())
    args.append(nc.dram_tensor("out_rows", (128, tiles, D), F32, kind="ExternalOutput").ap())
    build(nc, *args)
    r = run_bass_kernel_spmd(nc, [arrays], core_ids=[0])
    return np.ascontiguousarray(r.results[0]["out_rows"].transpose(1, 0, 2)).reshape(B, S, D)
```

```python
from contextlib import ExitStack

import concourse.bass as bass
from concourse import mybir

P = 128
F32 = mybir.dt.float32
I32 = mybir.dt.int32
U32 = mybir.dt.uint32
BF16 = mybir.dt.bfloat16
ALU = mybir.AluOpType
ACT = mybir.ActivationFunctionType
AX_X = mybir.AxisListType.X

EPS = 1e-5
MASKED = -3.0e38
RSQRT_MAGIC = float(0x5F3759DF)
ROW = 132
NOWHERE = 1 << 20
U = 3


def expert_blocks(tokens, experts):
    return 2 * tokens // P + experts - 1


def build(nc, x_rows, x_cols, ctx_cols, wq_t, wk_t, w_v, gate_t, w1_cols, w2_cols, out_rows, routed, picked):
    _, TILES, D = x_rows.shape
    T = TILES * P
    NE = gate_t.shape[1]
    HID = w1_cols.shape[2]
    HC = HID // P
    S = 64
    GT = 4
    GROUPS = TILES // GT
    GW = GT * P
    SCALE = 1.0 / D ** 0.5
    REGION = T + P
    BLOCKS = expert_blocks(T, NE)
    SPARE = BLOCKS - 2 * T // P
    TURNS = BLOCKS // U
    assert BLOCKS == TURNS * U

    with ExitStack() as ctx:
        def sb(name, shape, dt=F32):
            return ctx.enter_context(nc.sbuf_tensor(name, shape, dt))

        def sem(name):
            return ctx.enter_context(nc.semaphore(name))

        x_sb = sb("x_sb", [P, TILES, D])
        xT_sb = sb("xT_sb", [P, T])
        cT_sb = sb("cT_sb", [P, T])
        wq_sb = sb("wq_sb", [P, D])
        wk_sb = sb("wk_sb", [P, D])
        wv_sb = sb("wv_sb", [P, D])
        gw_sb = sb("gw_sb", [P, NE])
        w1_sb = sb("w1_sb", [P, NE + 1, HID])
        w2_sb = sb("w2_sb", [P, NE + 1, HC, D])
        ident = sb("ident", [P, P])
        causal = sb("causal", [P, S])
        ones_f = sb("ones_f", [P, 1])
        ones_b = sb("ones_b", [P, P], BF16)
        before = sb("before", [P, P], BF16)
        rank_key = sb("rank_key", [P, GT, NE])
        region_start = sb("region_start", [P, GT, NE])
        block_no = sb("block_no", [1, BLOCKS])
        ones8 = sb("ones8", [1, NE])
        empty_row = sb("empty_row", [P, ROW])
        wq_c = sb("wq_c", [P, D])
        qk_w = sb("qk_w", [P, D])
        tT = sb("tT", [P, 2, GW])
        v_sb = sb("v_sb", [P, 2, GT, D])
        s_sb = sb("s_sb", [P, GT, S])
        s_max = sb("s_max", [P, GT])
        probs = sb("probs", [P, 2, GT, P])
        pT = sb("pT", [P, GT, P])
        rsum = sb("rsum", [P, GT])
        stat = sb("stat", [P, TILES, 6])
        mv1 = sb("mv1", [P, TILES, 2])
        mv2 = sb("mv2", [P, TILES, 2])
        rstd1 = sb("rstd1", [P, TILES])
        rstd2 = sb("rstd2", [P, TILES])
        ve = sb("ve", [P, TILES])
        newton = sb("newton", [P, TILES])
        x2 = sb("x2", [P, TILES, D])
        sent = sb("sent", [P, TILES, 2, ROW])
        x2nT = sb("x2nT", [P, T])
        logits = sb("logits", [P, GT, NE])
        first = sb("first", [P, GT, NE])
        second = sb("second", [P, GT, NE])
        rest = sb("rest", [P, GT, NE])
        tmp = sb("tmp", [P, GT, NE])
        m1 = sb("m1", [P, TILES])
        m2 = sb("m2", [P, TILES])
        key = sb("key", [P, GT])
        chosen = sb("chosen", [P, GT, NE], BF16)
        chosen_above = sb("chosen_above", [P, TILES + 1, NE], BF16)
        place_f = sb("place_f", [P, GT, 2])
        place = sb("place", [P, TILES, 2], I32)
        count_i = sb("count_i", [1, NE], I32)
        nblk_i = sb("nblk_i", [1, NE], I32)
        nblk = sb("nblk", [1, NE])
        cum = sb("cum", [1, NE])
        skip = sb("skip", [1, NE])
        passed = sb("passed", [1, BLOCKS, NE])
        passed2 = sb("passed2", [1, BLOCKS, NE])
        of_f = sb("of_f", [1, BLOCKS])
        row_f = sb("row_f", [1, BLOCKS])
        block_expert = sb("block_expert", [1, BLOCKS], I32)
        block_row = sb("block_row", [1, BLOCKS], I32)
        tail_row = sb("tail_row", [1, NE], I32)
        dm = sb("dm", [P, TILES])
        e2 = sb("e2", [P, TILES])
        g1 = sb("g1", [P, TILES])
        g2 = sb("g2", [P, TILES])
        h_sb = sb("h_sb", [P, 2, HC, GW])
        acc = sb("acc", [P, TILES, D])
        xg = sb("xg", [P, U, ROW])
        xgT = sb("xgT", [P, U, P])
        w1_blk = sb("w1_blk", [P, U, HID])
        hT = sb("hT", [P, U, HID])
        y_sb = sb("y_sb", [P, U, D])
        dest = sb("dest", [P, BLOCKS], U32)
        y_in = sb("y_in", [P, 2, TILES, D])

        banks = [ctx.enter_context(nc.psum_tensor(f"bank{i}", [P, 512], F32)) for i in range(8)]
        ps_proj, ps_h0, ps_s, ps_tr, ps_o, ps_route, ps_h1, ps_y = banks
        ps_up = (ps_h0, ps_h1)
        ps_xg, ps_hT, ps_yb = ps_tr, (banks[0], banks[1], banks[2]), (banks[4], banks[6], banks[7])

        ld_w = sem("ld_w")
        ld_x = [sem(f"ld_x{i}") for i in range(GROUPS)]
        ld_xT = [sem(f"ld_xT{i}") for i in range(GROUPS)]
        ld_cT = [sem(f"ld_cT{i}") for i in range(GROUPS)]
        ld_shared = sem("ld_shared")
        ld_experts = sem("ld_experts")
        consts_done = sem("consts_done")
        route_consts = sem("route_consts")
        wq_centred = sem("wq_centred")
        qkw_psum = sem("qkw_psum")
        qkw_done = sem("qkw_done")
        t_psum = sem("t_psum")
        t_sbuf = sem("t_sbuf")
        v_psum = sem("v_psum")
        v_sbuf = sem("v_sbuf")
        s_psum = sem("s_psum")
        s_read = sem("s_read")
        s_ready = sem("s_ready")
        exp_done = sem("exp_done")
        tr_psum = sem("tr_psum")
        tr_sbuf = sem("tr_sbuf")
        o_psum = sem("o_psum")
        rsum_read = sem("rsum_read")
        x2_done = sem("x2_done")
        x2n_done = sem("x2n_done")
        l_psum = sem("l_psum")
        l_read = sem("l_read")
        chosen_done = sem("chosen_done")
        rank_psum = sem("rank_psum")
        rank_read = sem("rank_read")
        placed = sem("placed")
        sent_done = sem("sent_done")
        count_psum = sem("count_psum")
        tails_known = sem("tails_known")
        blocks_known = sem("blocks_known")
        tails_done = sem("tails_done")
        dm_done = sem("dm_done")
        e2_done = sem("e2_done")
        h_psum = sem("h_psum")
        h_sbuf = sem("h_sbuf")
        y_psum = sem("y_psum")
        acc_done = sem("acc_done")
        ld_blk = [sem(f"ld_blk{u}") for u in range(U)]
        xg_psum = sem("xg_psum")
        xgT_done = sem("xgT_done")
        w1_ready = sem("w1_ready")
        hT_psum = sem("hT_psum")
        hT_done = sem("hT_done")
        yb_psum = sem("yb_psum")
        yb_ready = sem("yb_ready")
        yb_sent = [sem(f"yb_sent{u}") for u in range(U)]
        ld_y = [sem(f"ld_y{g}") for g in range(GROUPS)]
        out_done = sem("out_done")
        stored = sem("stored")
        dve_step = sem("dve_step")
        pool_step = sem("pool_step")

        def all_turns(eng, body):
            for u in range(U):
                body(u, 0, u)
            with eng.Fori(1, TURNS - 1) as turn:
                for u in range(U):
                    body(turn * U + u, turn, u)
            for u in range(U):
                body((TURNS - 1) * U + u, TURNS - 1, u)

        block = ctx.enter_context(nc.Block())

        @block.sync
        def _(sp):
            sp.dma_start(wq_sb[:], wq_t).then_inc(ld_w, 16)
            sp.dma_start(wk_sb[:], wk_t).then_inc(ld_w, 16)
            sp.dma_start(wv_sb[:], w_v).then_inc(ld_w, 16)
            sp.dma_start(gw_sb[:], gate_t).then_inc(ld_w, 16)
            for g in range(GROUPS):
                cols, tiles = slice(g * GW, (g + 1) * GW), slice(g * GT, (g + 1) * GT)
                sp.dma_start(xT_sb[:, cols], x_cols[:, cols]).then_inc(ld_xT[g], 16)
                sp.dma_start(cT_sb[:, cols], ctx_cols[:, cols]).then_inc(ld_cT[g], 16)
                sp.dma_start(x_sb[:, tiles, :], x_rows[:, tiles, :]).then_inc(ld_x[g], 16)
            sp.dma_start(w1_sb[:, NE, :], w1_cols[:, NE, :]).then_inc(ld_shared, 16)
            sp.dma_start(w2_sb[:, NE, :, :], w2_cols[:, NE, :, :]).then_inc(ld_shared, 16)
            sp.wait_ge(route_consts, 1)
            for k in range(SPARE):
                r = NE * REGION + k * P
                sp.dma_start(routed[r:r + P, :], empty_row[:]).then_inc(tails_done, 16)
            sp.dma_start(w1_sb[:, 0:NE, :], w1_cols[:, 0:NE, :]).then_inc(ld_experts, 16)
            sp.dma_start(w2_sb[:, 0:NE, :, :], w2_cols[:, 0:NE, :, :]).then_inc(ld_experts, 16)
            sp.wait_ge(tails_known, 1)
            for e in range(NE):
                r = sp.value_load(tail_row[0:1, e:e + 1], min_val=0, max_val=NE * REGION - P)
                sp.dma_start(routed[bass.ds(r, P), :], empty_row[:]).then_inc(tails_done, 16)
            sp.wait_ge(blocks_known, 1)
            sp.wait_ge(tails_done, 16 * (SPARE + NE))
            sp.wait_ge(sent_done, 16 * 2 * TILES)

            def load_block(b, turn, u):
                if not (isinstance(turn, int) and turn == 0):
                    sp.wait_ge(w1_ready, b - U + 1)
                r = sp.value_load(block_row[0:1, bass.ds(b, 1)], min_val=0, max_val=(NE * REGION + (SPARE - 1) * P))
                sp.dma_start(xg[:, u, :], routed[bass.ds(r, P), :]).then_inc(ld_blk[u], 16)

            all_turns(sp, load_block)
            for u in range(U):
                sp.wait_ge(yb_sent[u], 16 * TURNS)
            for g in range(GROUPS):
                for k in range(2):
                    r = k * T + g * GW
                    sp.dma_start(y_in[:, k, g * GT:(g + 1) * GT, :],
                                 picked[r:r + GW, :].rearrange("(i p) d -> p i d", p=P)).then_inc(ld_y[g], 16)
            for g in range(GROUPS):
                tiles = slice(g * GT, (g + 1) * GT)
                sp.wait_ge(out_done, g + 1)
                sp.dma_start(out_rows[:, tiles, :], acc[:, tiles, :]).then_inc(stored, 16)
            sp.wait_ge(stored, 16 * GROUPS)

        @block.gpsimd
        def _(pool):
            steps = [0]

            def link(ins):
                steps[0] += 1
                ins.then_inc(pool_step, 1)
                pool.wait_ge(pool_step, steps[0])

            G = nc.gpsimd
            link(G.memset(ident[:], 0.0))
            link(G.affine_select(out=ident[:], in_=ident[:], compare_op=ALU.not_equal, fill=1.0, base=0,
                                 pattern=[[-1, P]], channel_multiplier=1))
            link(G.memset(causal[:], 0.0))
            for b in range(2):
                rows = slice(b * S, (b + 1) * S)
                link(G.affine_select(out=causal[rows, :], in_=causal[rows, :], compare_op=ALU.is_ge,
                                     fill=MASKED, base=0, pattern=[[-1, S]], channel_multiplier=1))
            link(G.memset(ones_f[:], 1.0))
            G.memset(probs[:], 0.0).then_inc(consts_done, 1)
            pool.wait_ge(consts_done, 1)
            link(G.iota(rank_key[:], pattern=[[0, GT], [-1, NE]], base=NE, channel_multiplier=0,
                        allow_small_or_imprecise_dtypes=True))
            link(G.iota(region_start[:], pattern=[[0, GT], [REGION, NE]], base=0, channel_multiplier=0,
                        allow_small_or_imprecise_dtypes=True))
            link(G.iota(block_no[:], pattern=[[1, BLOCKS]], base=0, channel_multiplier=0,
                        allow_small_or_imprecise_dtypes=True))
            link(G.memset(ones8[:], 1.0))
            link(G.memset(ones_b[:], 1.0))
            link(G.affine_select(out=before[:], in_=ones_b[:], compare_op=ALU.is_gt, fill=0.0, base=0,
                                 pattern=[[1, P]], channel_multiplier=-1))
            link(G.memset(chosen_above[:, 0, :], 0.0))
            link(G.memset(empty_row[:], 0.0))
            link(G.iota(empty_row[:, D:D + 1].bitcast(I32), pattern=[[0, 1]], base=NOWHERE, channel_multiplier=0))
            link(G.memset(sent[:, :, :, D + 1:ROW], 0.0))
            G.iota(sent[:, :, :, D].bitcast(I32), pattern=[[P, TILES], [T, 2]], base=0,
                   channel_multiplier=1).then_inc(route_consts, 1)
            for g in range(GROUPS):
                pool.wait_ge(placed, g + 1)
                for i in range(g * GT, (g + 1) * GT):
                    for k in range(2):
                        G.indirect_dma_start(routed, bass.IndirectOffsetOnAxis(place[:, i, k:k + 1].bitcast(U32), 0),
                                             sent[:, i, k, :], None).then_inc(sent_done, 16)

            for b in range(BLOCKS):
                u = b % U
                pool.wait_ge(yb_ready, b + 1)
                G.indirect_dma_start(picked, bass.IndirectOffsetOnAxis(dest[:, b:b + 1], 0), y_sb[:, u, :], None,
                                     bounds_check=2 * T - 1, oob_is_err=False).then_inc(yb_sent[u], 16)

        @block.tensor
        def _(pe):
            mm = nc.tensor.matmul
            pe.wait_ge(wq_centred, 1)
            mm(ps_o[:, 0:D], wq_c[:], wk_sb[:], start=True, stop=True).then_inc(qkw_psum, 1)
            pe.wait_ge(consts_done, 1)

            def project(g):
                pe.wait_ge(ld_xT[g], 16)
                if g == 0:
                    pe.wait_ge(qkw_done, 1)
                else:
                    pe.wait_ge(v_sbuf, g)
                mm(ps_proj[:], qk_w[:], xT_sb[:, g * GW:(g + 1) * GW], start=True, stop=True).then_inc(t_psum, 1)
                pe.wait_ge(ld_cT[g], 16)
                pe.wait_ge(t_sbuf, g + 1)
                for i in range(GT):
                    at = g * GW + i * P
                    last = mm(ps_proj[:, i * D:(i + 1) * D], cT_sb[:, at:at + P], wv_sb[:], start=True, stop=True)
                last.then_inc(v_psum, 1)

            def score(g):
                if g:
                    pe.wait_ge(rsum_read, g)
                for i in range(GT):
                    for b in range(2):
                        at = i * P + b * S
                        last = mm(ps_s[b * S:(b + 1) * S, i * S:(i + 1) * S], tT[:, g % 2, at:at + S],
                                  cT_sb[:, g * GW + at:g * GW + at + S], start=True, stop=True)
                last.then_inc(s_psum, 1)

            def attend(g):
                pe.wait_ge(exp_done, g + 1)
                if g:
                    pe.wait_ge(tr_sbuf, 2 * g)
                for i in range(GT):
                    last = nc.tensor.transpose(ps_tr[:, i * P:(i + 1) * P], probs[:, g % 2, i, :], ident[:])
                last.then_inc(tr_psum, 1)
                pe.wait_ge(tr_sbuf, 2 * g + 1)
                pe.wait_ge(v_sbuf, g + 1)
                if g:
                    pe.wait_ge(x2_done, g)
                for i in range(GT):
                    mm(ps_s[:, GT * S + i:GT * S + i + 1], pT[:, i, :], ones_f[:], start=True, stop=True)
                    last = mm(ps_o[:, i * D:(i + 1) * D], pT[:, i, :], v_sb[:, g % 2, i, :], start=True, stop=True)
                last.then_inc(o_psum, 1)

            def gate(g):
                pe.wait_ge(x2n_done, g + 1)
                pe.wait_ge(tr_sbuf, 2 * g + 1)
                for i in range(GT):
                    last = nc.tensor.transpose(ps_tr[:, i * P:(i + 1) * P], sent[:, g * GT + i, 0, 0:D], ident[:])
                last.then_inc(tr_psum, 1)
                pe.wait_ge(tr_sbuf, 2 * g + 2)
                if g:
                    pe.wait_ge(rank_read, g)
                for i in range(GT):
                    t = g * GT + i
                    last = mm(ps_route[:, i * NE:(i + 1) * NE], x2nT[:, t * P:(t + 1) * P], gw_sb[:],
                              start=True, stop=True)
                last.then_inc(l_psum, 1)

            def rank(g):
                pe.wait_ge(chosen_done, g + 1)
                ranks = ps_route[:, GT * NE:2 * GT * NE]
                mm(ranks, before[:], chosen[:], start=True, stop=False)
                mm(ranks, ones_b[:], chosen_above[:, g * GT:(g + 1) * GT, :], start=False,
                   stop=True).then_inc(rank_psum, 1)

            def count():
                pe.wait_ge(rank_read, GROUPS)
                mm(ps_route[:, 0:NE], ones_b[:], chosen_above[:, TILES, :], start=True, stop=True).then_inc(count_psum, 1)

            def up(g):
                if g == 0:
                    pe.wait_ge(ld_shared, 32)
                for c in range(HC):
                    n = g * HC + c
                    if n >= 2:
                        pe.wait_ge(h_sbuf, n - 1)
                    mm(ps_up[n % 2][:], w1_sb[:, NE, c * P:(c + 1) * P], x2nT[:, g * GW:(g + 1) * GW],
                       start=True, stop=True).then_inc(h_psum, 1)

            def down(g):
                pe.wait_ge(h_sbuf, HC * (g + 1))
                if g:
                    pe.wait_ge(acc_done, g)
                for i in range(GT):
                    for c in range(HC):
                        last = mm(ps_y[:, i * D:(i + 1) * D], h_sb[:, g % 2, c, i * P:(i + 1) * P],
                                  w2_sb[:, NE, c, :], start=(c == 0), stop=(c == HC - 1))
                last.then_inc(y_psum, 1)

            project(0); score(0); project(1)
            attend(0); score(1); project(2)
            gate(0); attend(1); score(2); rank(0); project(3)
            gate(1); attend(2); score(3); rank(1); up(0)
            gate(2); attend(3); rank(2); up(1); down(0)
            gate(3); up(2); rank(3); count(); down(1); up(3); down(2); down(3)

            def turn_rows(b, turn, u):
                pe.wait_ge(ld_blk[u], 16 * (turn + 1))
                if not (isinstance(b, int) and b == 0):
                    pe.wait_ge(xgT_done, b)
                nc.tensor.transpose(ps_xg[:, 0:P], xg[:, u, 0:D], ident[:]).then_inc(xg_psum, 1)

            def block_up(b, u):
                pe.wait_ge(w1_ready, b + 1)
                for c in range(HC):
                    last = mm(ps_hT[u][:, c * P:(c + 1) * P], w1_blk[:, u, c * P:(c + 1) * P], xgT[:, u, :],
                              start=True, stop=True)
                last.then_inc(hT_psum, 1)

            def block_down(b, turn, u):
                e = pe.value_load(block_expert[0:1, bass.ds(b, 1)], min_val=0, max_val=NE)
                pe.wait_ge(hT_done, b + 1)
                if not (isinstance(turn, int) and turn == 0):
                    pe.wait_ge(yb_ready, b - U + 1)
                for c in range(HC):
                    last = mm(ps_yb[u][:, 0:D], hT[:, u, c * P:(c + 1) * P],
                              w2_sb[:, bass.ds(e, 1), c, :].rearrange("p a d -> p (a d)"),
                              start=(c == 0), stop=(c == HC - 1))
                last.then_inc(yb_psum, 1)

            pe.wait_ge(blocks_known, 1)
            pe.wait_ge(ld_experts, 32)
            pe.wait_ge(acc_done, GROUPS)
            turn_rows(0, 0, 0)
            turn_rows(1, 0, 1)
            block_up(0, 0)

            def block(b, turn, u):
                last_turn = isinstance(b, int)
                if not last_turn or b + 2 < BLOCKS:
                    turn_rows(b + 2, turn + (u + 2) // U, (u + 2) % U)
                if not last_turn or b + 1 < BLOCKS:
                    block_up(b + 1, (u + 1) % U)
                block_down(b, turn, u)

            all_turns(pe, block)

        @block.scalar
        def _(act):
            A = nc.scalar.activation
            act.wait_ge(qkw_psum, 1)
            A(qk_w[:], ps_o[:, 0:D], ACT.Copy, scale=SCALE).then_inc(qkw_done, 1)
            act.wait_ge(consts_done, 1)

            def evacuate_projections(g):
                act.wait_ge(t_psum, g + 1)
                if g >= 2:
                    act.wait_ge(s_psum, g - 1)
                A(tT[:, g % 2, :], ps_proj[:], ACT.Copy).then_inc(t_sbuf, 1)
                act.wait_ge(v_psum, g + 1)
                if g >= 2:
                    act.wait_ge(o_psum, g - 1)
                A(v_sb[:, g % 2, :, :], ps_proj[:].rearrange("p (i d) -> p i d", i=GT), ACT.Copy).then_inc(v_sbuf, 1)

            def softmax_exp(g):
                act.wait_ge(s_ready, g + 1)
                if g >= 2:
                    act.wait_ge(tr_psum, 2 * (g - 2) + 1)
                for b in range(2):
                    rows = slice(b * S, (b + 1) * S)
                    last = A(probs[rows, g % 2, :, b * S:(b + 1) * S], s_sb[rows, :, :], ACT.Exp)
                last.then_inc(exp_done, 1)

            def evacuate_pT(g):
                act.wait_ge(tr_psum, 2 * g + 1)
                if g:
                    act.wait_ge(o_psum, g)
                A(pT[:], ps_tr[:].rearrange("p (i q) -> p i q", i=GT), ACT.Copy).then_inc(tr_sbuf, 1)

            def evacuate_x2nT(g):
                act.wait_ge(tr_psum, 2 * g + 2)
                A(x2nT[:, g * GW:(g + 1) * GW], ps_tr[:], ACT.Copy).then_inc(tr_sbuf, 1)

            def hidden(g):
                for c in range(HC):
                    act.wait_ge(h_psum, HC * g + c + 1)
                    if g >= 2 and c == 0:
                        act.wait_ge(y_psum, g - 1)
                    A(h_sb[:, g % 2, c, :], ps_up[(g * HC + c) % 2][:], ACT.Silu).then_inc(h_sbuf, 1)

            evacuate_projections(0); evacuate_projections(1)
            softmax_exp(0); evacuate_pT(0); evacuate_projections(2)
            softmax_exp(1); evacuate_x2nT(0); evacuate_pT(1); evacuate_projections(3)
            softmax_exp(2); evacuate_x2nT(1); evacuate_pT(2)
            softmax_exp(3); hidden(0); evacuate_x2nT(2); evacuate_pT(3)
            hidden(1); evacuate_x2nT(3); hidden(2); hidden(3)
            act.wait_ge(dm_done, 1)
            A(e2[:], dm[:], ACT.Exp).then_inc(e2_done, 1)

            def block_hidden(b, turn, u):
                act.wait_ge(hT_psum, b + 1)
                A(hT[:, u, :], ps_hT[u][:], ACT.Silu).then_inc(hT_done, 1)

            all_turns(act, block_hidden)

        @block.vector
        def _(dve):
            steps = [0]

            def link(ins):
                steps[0] += 1
                ins.then_inc(dve_step, 1)
                dve.wait_ge(dve_step, steps[0])

            V = nc.vector

            def rsqrt(dst, var, y, v):
                link(V.tensor_scalar(v, var, EPS, None, ALU.add))
                link(V.tensor_scalar(dst.bitcast(I32), v.bitcast(I32), 1, None, ALU.logical_shift_right))
                link(V.tensor_scalar(dst.bitcast(I32), dst.bitcast(I32), -1.0, RSQRT_MAGIC, ALU.mult, ALU.add))
                for _ in range(3):
                    link(V.tensor_tensor(y, v, dst, ALU.mult))
                    link(V.scalar_tensor_tensor(y, y, -0.5, dst, ALU.mult, ALU.mult))
                    link(V.scalar_tensor_tensor(dst, y, 1.5, dst, ALU.add, ALU.mult))

            def statistics(src, mv, tiles):
                for i in tiles:
                    last = V.bn_stats(stat[:, i, :], src[:, i, :])
                link(last)
                for i in tiles:
                    last = V.bn_aggr(mv[:, i, :], stat[:, i, :])
                link(last)

            def norm1(g0, g1):
                for g in range(g0, g1):
                    dve.wait_ge(ld_x[g], 16)
                tiles = slice(g0 * GT, g1 * GT)
                statistics(x_sb, mv1, range(g0 * GT, g1 * GT))
                rsqrt(rstd1[:, tiles], mv1[:, tiles, 1], newton[:, tiles], ve[:, tiles])

            def softmax(g):
                dve.wait_ge(s_psum, g + 1)
                if g:
                    dve.wait_ge(exp_done, g)
                for i in range(GT):
                    last = V.scalar_tensor_tensor(s_sb[:, i, :], ps_s[:, i * S:(i + 1) * S],
                                                  rstd1[:, g * GT + i:g * GT + i + 1], causal[:], ALU.mult, ALU.add)
                last.then_inc(s_read, 1)
                dve.wait_ge(s_read, g + 1)
                link(V.reduce_max(s_max[:], s_sb[:], AX_X))
                V.tensor_tensor(s_sb[:], s_sb[:], s_max[:].unsqueeze(2).to_broadcast([P, GT, S]),
                                ALU.subtract).then_inc(s_ready, 1)

            def residual(g):
                dve.wait_ge(o_psum, g + 1)
                V.reciprocal(rsum[:], ps_s[:, GT * S:GT * S + GT]).then_inc(rsum_read, 1)
                dve.wait_ge(rsum_read, g + 1)
                for i in range(GT):
                    last = V.scalar_tensor_tensor(x2[:, g * GT + i, :], ps_o[:, i * D:(i + 1) * D], rsum[:, i:i + 1],
                                                  x_sb[:, g * GT + i, :], ALU.mult, ALU.add)
                last.then_inc(x2_done, 1)
                dve.wait_ge(x2_done, g + 1)

            def norm2(g):
                tiles = slice(g * GT, (g + 1) * GT)
                statistics(x2, mv2, range(g * GT, (g + 1) * GT))
                rsqrt(rstd2[:, tiles], mv2[:, tiles, 1], newton[:, tiles], ve[:, tiles])
                for i in range(g * GT, (g + 1) * GT):
                    last = V.tensor_scalar(sent[:, i, 0, 0:D], x2[:, i, :], mv2[:, i, 0:1], rstd2[:, i:i + 1],
                                           ALU.subtract, ALU.mult)
                last.then_inc(x2n_done, 1)

            def wide(a):
                return a.unsqueeze(2).to_broadcast([P, GT, NE])

            def pick(one_hot, values, top):
                link(V.reduce_max(top, values[:], AX_X))
                link(V.tensor_tensor(tmp[:], values[:], wide(top), ALU.is_equal))
                link(V.tensor_tensor(tmp[:], tmp[:], rank_key[:], ALU.mult))
                link(V.reduce_max(key[:], tmp[:], AX_X))
                link(V.tensor_tensor(one_hot[:], tmp[:], wide(key[:]), ALU.is_equal))

            def choose(g):
                tiles = slice(g * GT, (g + 1) * GT)
                dve.wait_ge(x2n_done, g + 1)
                V.tensor_copy(sent[:, tiles, 1, 0:D], sent[:, tiles, 0, 0:D])
                dve.wait_ge(l_psum, g + 1)
                V.tensor_copy(logits[:], ps_route[:, 0:GT * NE].rearrange("p (i e) -> p i e", e=NE)).then_inc(l_read, 1)
                dve.wait_ge(l_read, g + 1)
                pick(first, logits, m1[:, tiles])
                link(V.scalar_tensor_tensor(rest[:], first[:], MASKED, logits[:], ALU.mult, ALU.add))
                pick(second, rest, m2[:, tiles])
                link(V.tensor_tensor(chosen[:], first[:], second[:], ALU.add))
                for i in range(GT):
                    t = g * GT + i
                    last = V.tensor_tensor(chosen_above[:, t + 1, :], chosen_above[:, t, :], chosen[:, i, :], ALU.add)
                    if i < GT - 1:
                        link(last)
                last.then_inc(chosen_done, 1)
                dve.wait_ge(chosen_done, g + 1)

            def assign(g):
                dve.wait_ge(rank_psum, g + 1)
                ranks = ps_route[:, GT * NE:2 * GT * NE].rearrange("p (i e) -> p i e", e=NE)
                V.tensor_tensor(rest[:], ranks, region_start[:], ALU.add).then_inc(rank_read, 1)
                dve.wait_ge(rank_read, g + 1)
                for k, one_hot in enumerate((first, second)):
                    link(V.tensor_tensor(tmp[:], one_hot[:], rest[:], ALU.mult))
                    link(V.reduce_sum(place_f[:, :, k], tmp[:], AX_X))
                V.tensor_copy(place[:, g * GT:(g + 1) * GT, :], place_f[:]).then_inc(placed, 1)

            def plan_blocks():
                dve.wait_ge(count_psum, 1)
                counts = ps_route[0:1, 0:NE]
                link(V.tensor_scalar(count_i[:], counts, float(P - 1), None, ALU.add))
                V.tensor_tensor(tail_row[:], counts, region_start[0:1, 0, :], ALU.add).then_inc(tails_known, 1)
                link(V.tensor_scalar(nblk_i[:], count_i[:], P.bit_length() - 1, None, ALU.logical_shift_right))
                link(V.tensor_copy(nblk[:], nblk_i[:]))
                link(V.tensor_tensor_scan(cum[:], ones8[:], nblk[:], 0.0, ALU.mult, ALU.add))
                link(V.tensor_scalar(skip[:], nblk[:], -float(P), float(REGION), ALU.mult, ALU.add))
                link(V.tensor_tensor(passed[:], block_no[:].unsqueeze(2).to_broadcast([1, BLOCKS, NE]),
                                     cum[:].unsqueeze(1).to_broadcast([1, BLOCKS, NE]), ALU.is_ge))
                link(V.reduce_sum(of_f[:], passed[:], AX_X))
                link(V.tensor_tensor(passed2[:], passed[:], skip[:].unsqueeze(1).to_broadcast([1, BLOCKS, NE]), ALU.mult))
                link(V.reduce_sum(row_f[:], passed2[:], AX_X))
                link(V.tensor_copy(block_expert[:], of_f[:]))
                V.scalar_tensor_tensor(block_row[:], block_no[:], float(P), row_f[:], ALU.mult,
                                       ALU.add).then_inc(blocks_known, 1)

            def add_shared(g):
                dve.wait_ge(y_psum, g + 1)
                tiles = slice(g * GT, (g + 1) * GT)
                V.tensor_tensor(acc[:, tiles, :], ps_y[:].rearrange("p (i d) -> p i d", i=GT), x2[:, tiles, :],
                                ALU.add).then_inc(acc_done, 1)

            dve.wait_ge(ld_w, 64)
            statistics(wq_sb[:].unsqueeze(1), mv1, range(1))
            V.tensor_scalar(wq_c[:], wq_sb[:], mv1[:, 0, 0:1], None, ALU.subtract).then_inc(wq_centred, 1)
            dve.wait_ge(wq_centred, 1)
            norm1(0, 1)
            dve.wait_ge(consts_done, 1)
            softmax(0)
            norm1(1, GROUPS)
            dve.wait_ge(route_consts, 1)
            residual(0); norm2(0)
            softmax(1); residual(1); choose(0); norm2(1)
            softmax(2); assign(0); residual(2); choose(1); norm2(2)
            softmax(3); assign(1); residual(3); choose(2); norm2(3)
            assign(2); add_shared(0); choose(3); assign(3); plan_blocks()
            V.tensor_tensor(dm[:], m2[:], m1[:], ALU.subtract).then_inc(dm_done, 1)
            add_shared(1); add_shared(2); add_shared(3)
            dve.wait_ge(e2_done, 1)
            link(V.tensor_scalar(g1[:], e2[:], 1.0, None, ALU.add))
            link(V.reciprocal(g1[:], g1[:]))
            link(V.tensor_tensor(g2[:], e2[:], g1[:], ALU.mult))
            dve.wait_ge(blocks_known, 1)
            dve.wait_ge(ld_experts, 32)

            def stage(b, u):
                e = V.value_load(block_expert[0:1, bass.ds(b, 1)], min_val=0, max_val=NE)
                dve.wait_ge(xg_psum, b + 1)
                V.tensor_copy(xgT[:, u, :], ps_xg[:, 0:P]).then_inc(xgT_done, 1)
                V.tensor_copy(w1_blk[:, u, :], w1_sb[:, bass.ds(e, 1), :].rearrange("p a h -> p (a h)"))
                V.tensor_copy(dest[:, bass.ds(b, 1)], xg[:, u, D:D + 1].bitcast(U32)).then_inc(w1_ready, 1)

            stage(0, 0)
            stage(1, 1)

            def block(b, turn, u):
                if not isinstance(b, int) or b + 2 < BLOCKS:
                    stage(b + 2, (u + 2) % U)
                dve.wait_ge(yb_psum, b + 1)
                if not (isinstance(turn, int) and turn == 0):
                    dve.wait_ge(yb_sent[u], 16 * turn)
                V.tensor_copy(y_sb[:, u, :], ps_yb[u][:, 0:D]).then_inc(yb_ready, 1)

            all_turns(dve, block)
            for g in range(GROUPS):
                dve.wait_ge(ld_y[g], 32)
                for k, gate in enumerate((g1, g2)):
                    for i in range(g * GT, (g + 1) * GT):
                        last = V.scalar_tensor_tensor(acc[:, i, :], y_in[:, k, i, :], gate[:, i:i + 1], acc[:, i, :],
                                                      ALU.mult, ALU.add)
                    if k == 0:
                        link(last)
                last.then_inc(out_done, 1)


def kernel(x, ctx_1024, L0_xattn_w_q, L0_xattn_w_k, L0_xattn_w_v, L0_ffn_shared_w1, L0_ffn_shared_w2,
           L0_ffn_experts_w1, L0_ffn_experts_w2, L0_ffn_gate_w):
    import numpy as np
    import concourse.bacc as bacc
    from concourse.bass_utils import run_bass_kernel_spmd

    B, S, D = x.shape
    tiles = B * S // P
    HID = L0_ffn_shared_w1.shape[0]
    NE = L0_ffn_gate_w.shape[0]
    w1 = np.concatenate([np.asarray(L0_ffn_experts_w1), np.asarray(L0_ffn_shared_w1)[None]])
    w2 = np.concatenate([np.asarray(L0_ffn_experts_w2), np.asarray(L0_ffn_shared_w2)[None]])
    laid_out = {
        "x_rows": np.asarray(x).reshape(tiles, P, D).transpose(1, 0, 2),
        "x_cols": np.asarray(x).reshape(B * S, D).T,
        "ctx_cols": np.asarray(ctx_1024).reshape(B * S, D).T,
        "wq_t": np.asarray(L0_xattn_w_q).T,
        "wk_t": np.asarray(L0_xattn_w_k).T,
        "w_v": np.asarray(L0_xattn_w_v),
        "gate_t": np.asarray(L0_ffn_gate_w).T,
        "w1_cols": w1.transpose(2, 0, 1),
        "w2_cols": w2.transpose(2, 0, 1).reshape(HID // P, P, NE + 1, D).transpose(1, 2, 0, 3),
    }
    nc = bacc.Bacc("TRN2", target_bir_lowering=False, num_devices=1)
    arrays, args = {}, []
    for name, a in laid_out.items():
        arrays[name] = np.ascontiguousarray(a)
        args.append(nc.dram_tensor(name, a.shape, mybir.dt.from_np(a.dtype), kind="ExternalInput").ap())
    args.append(nc.dram_tensor("out_rows", (P, tiles, D), F32, kind="ExternalOutput").ap())
    spare = expert_blocks(B * S, NE) - 2 * B * S // P
    args.append(nc.dram_tensor("routed", (NE * (B * S + P) + spare * P, ROW), F32, kind="Internal").ap())
    args.append(nc.dram_tensor("picked", (2 * B * S, D), F32, kind="Internal").ap())
    build(nc, *args)
    r = run_bass_kernel_spmd(nc, [arrays], core_ids=[0])
    return np.ascontiguousarray(r.results[0]["out_rows"].transpose(1, 0, 2)).reshape(B, S, D)
```

```python
from contextlib import ExitStack

import concourse.bass as bass
from concourse import mybir

P = 128
F32 = mybir.dt.float32
I32 = mybir.dt.int32
U32 = mybir.dt.uint32
BF16 = mybir.dt.bfloat16
ALU = mybir.AluOpType
ACT = mybir.ActivationFunctionType
AX_X = mybir.AxisListType.X

EPS = 1e-5
MASKED = -1.0e35
TAKEN = -3.0e38
RSQRT_MAGIC = float(0x5F3759DF)
ROW = 132
NOWHERE = 1 << 20
EARLY = 6
BESIDE = (2, 2, 1, 1)
U = 3


def expert_blocks(tokens, experts):
    return 2 * tokens // P + experts - 1


def build(nc, x_rows, x_cols, ctx_cols, w_small, w1_cols, w2_cols, out_rows, routed, picked):
    _, TILES, D = x_rows.shape
    T = TILES * P
    NE = w1_cols.shape[1] - 1
    HID = w1_cols.shape[2]
    HC = HID // P
    S = 64
    GT = 8
    GROUPS = TILES // GT
    QT = 4
    QUADS = TILES // QT
    QW = QT * P
    QG = GT // QT
    SCALE = 1.0 / D ** 0.5
    REGION = T + P
    BLOCKS = expert_blocks(T, NE)
    SPARE = BLOCKS - 2 * T // P
    TURNS = BLOCKS // U
    assert BLOCKS == TURNS * U

    with ExitStack() as ctx:
        def sb(name, shape, dt=F32):
            return ctx.enter_context(nc.sbuf_tensor(name, shape, dt))

        def sem(name):
            return ctx.enter_context(nc.semaphore(name))

        x_sb = sb("x_sb", [P, TILES, D])
        xT_sb = sb("xT_sb", [P, T])
        cT_sb = sb("cT_sb", [P, T])
        w_sb = sb("w_sb", [P, w_small.shape[1]])
        wq_sb, wk_sb, wv_sb = (w_sb[:, k * D:(k + 1) * D] for k in range(3))
        gw_sb = w_sb[:, 3 * D:3 * D + NE]
        w1_sb = sb("w1_sb", [P, NE + 1, HID])
        w2_sb = sb("w2_sb", [P, NE + 1, HC, D])
        ident = sb("ident", [P, P])
        ident_b = sb("ident_b", [P, P], BF16)
        causal = sb("causal", [P, S], BF16)
        centre = sb("centre", [P, P])
        ones_b = sb("ones_b", [P, P], BF16)
        before = sb("before", [P, P], BF16)
        rank_key = sb("rank_key", [P, GT, NE])
        region_start = sb("region_start", [P, GT, NE])
        block_no = sb("block_no", [1, BLOCKS])
        ones8 = sb("ones8", [1, NE])
        empty_row = sb("empty_row", [P, ROW])
        wq_c = sb("wq_c", [P, D])
        qk_w = sb("qk_w", [P, D])
        tT = sb("tT", [P, T])
        v_sb = sb("v_sb", [P, TILES, D])
        s_sb = sb("s_sb", [P, GROUPS, GT, S])
        s_max = sb("s_max", [P, GT])
        probs = sb("probs", [P, 2, GT, P])
        pT = sb("pT", [P, GT, P])
        part = sb("part", [P, GT, S])
        sums = sb("sums", [P, GROUPS, GT])
        rsum = sb("rsum", [P, GT])
        shift2 = sb("shift2", [P, TILES])
        stat = sb("stat", [P, TILES, 6])
        mv1 = sb("mv1", [P, TILES, 2])
        mv2 = sb("mv2", [P, TILES, 2])
        rstd1 = sb("rstd1", [P, TILES])
        rstd2 = sb("rstd2", [P, TILES])
        ve = sb("ve", [P, TILES])
        newton = sb("newton", [P, TILES])
        x2 = sb("x2", [P, TILES, D])
        sent = sb("sent", [P, TILES, 2, ROW])
        x2T = sb("x2T", [P, GT * P])
        x2nT = sb("x2nT", [P, T])
        gw_c = sb("gw_c", [P, NE])
        first = sb("first", [P, GT, NE])
        second = sb("second", [P, GT, NE])
        rest = sb("rest", [P, GT, NE])
        tmp = sb("tmp", [P, GT, NE])
        m1 = sb("m1", [P, GT])
        m2 = sb("m2", [P, GT])
        key1 = sb("key1", [P, GT])
        key2 = sb("key2", [P, GT])
        best_is_low = sb("best_is_low", [P, TILES])
        place_sum = sb("place_sum", [P, GT])
        chosen = sb("chosen", [P, TILES, NE], BF16)
        place_high = sb("place_high", [P, GT])
        place = sb("place", [P, TILES, 2], I32)
        count_i = sb("count_i", [1, NE], I32)
        nblk_i = sb("nblk_i", [1, NE], I32)
        nblk = sb("nblk", [1, NE])
        cum = sb("cum", [1, NE])
        skip = sb("skip", [1, NE])
        passed = sb("passed", [1, BLOCKS, NE])
        passed2 = sb("passed2", [1, BLOCKS, NE])
        of_f = sb("of_f", [1, BLOCKS])
        row_f = sb("row_f", [1, BLOCKS])
        block_expert = sb("block_expert", [1, BLOCKS], I32)
        block_row = sb("block_row", [1, BLOCKS], I32)
        tail_row = sb("tail_row", [1, NE], I32)
        high_needed = sb("high_needed", [1, BLOCKS], I32)
        low_done = sb("low_done", [1, 1], I32)
        mark_only = sb("mark_only", [1, 1])
        table_loaded = sb("table_loaded", [1, 1])
        dm = sb("dm", [P, TILES])
        dm2 = sb("dm2", [P, TILES, 2])
        e2 = sb("e2", [P, TILES, 2])
        e_sum = sb("e_sum", [P, TILES])
        gates = sb("gates", [P, TILES, 2])
        h_sb = sb("h_sb", [P, 2, HC, QW])
        acc = sb("acc", [P, TILES, D])
        xg = sb("xg", [P, U, ROW])
        xgT = sb("xgT", [P, U, P])
        w1_blk = sb("w1_blk", [P, U, HID])
        hT = sb("hT", [P, U, HID])
        y_sb = sb("y_sb", [P, U, D])
        goes_to = sb("goes_to", [P, BLOCKS], U32)
        y_in = [a[:].rearrange("p (i d) -> p i d", d=D) for a in (xT_sb, cT_sb)]

        banks = [ctx.enter_context(nc.psum_tensor(f"bank{i}", [P, 512], F32)) for i in range(8)]
        ps_t = (banks[0], banks[5])
        ps_s = (banks[1], banks[6])
        ps_pT = ps_x2nT = banks[2:4]
        ps_x2T = ((banks[1], banks[7]), banks[2:4])
        ps_o, ps_route, ps_count = banks[4:6], banks[6], banks[0]
        ps_v = (banks[7], banks[1], banks[0], banks[7])
        ps_up, ps_y = (banks[1], banks[7]), banks[4:6]
        ps_xg, ps_hT, ps_yb = banks[2], (banks[0], banks[3], banks[7]), banks[4:7]

        ld_w = sem("ld_w")
        ld_x = [sem(f"ld_x{i}") for i in range(QUADS)]
        ld_xT = [sem(f"ld_xT{i}") for i in range(QUADS)]
        ld_cT = [sem(f"ld_cT{i}") for i in range(QUADS)]
        ld_shared = sem("ld_shared")
        ld_experts = sem("ld_experts")
        consts_done = sem("consts_done")
        route_consts = sem("route_consts")
        wq_centred = sem("wq_centred")
        qkw_psum = sem("qkw_psum")
        qkw_done = sem("qkw_done")
        t_psum = sem("t_psum")
        t_sbuf = sem("t_sbuf")
        v_psum = sem("v_psum")
        v_sbuf = sem("v_sbuf")
        s_psum = sem("s_psum")
        s_read = sem("s_read")
        s_ready = sem("s_ready")
        exp_done = sem("exp_done")
        pT_psum = sem("pT_psum")
        pT_done = sem("pT_done")
        x2T_psum = sem("x2T_psum")
        x2T_done = sem("x2T_done")
        gw_psum = sem("gw_psum")
        gw_done = sem("gw_done")
        copied = sem("copied")
        x2nT_psum = sem("x2nT_psum")
        o_psum = sem("o_psum")
        sums_known = sem("sums_known")
        x2_done = sem("x2_done")
        ident_done = sem("ident_done")
        guess1_done = sem("guess1_done")
        norm1_known = sem("norm1_known")
        guess2_done = sem("guess2_done")
        norm2_known = [sem(f"norm2_known{g}") for g in range(GROUPS)]
        x2n_done = sem("x2n_done")
        x2nT_done = sem("x2nT_done")
        l_psum = sem("l_psum")
        chosen_done = sem("chosen_done")
        rank_psum = sem("rank_psum")
        rank_read = sem("rank_read")
        placed = sem("placed")
        sent_low = sem("sent_low")
        sent_high = sem("sent_high")
        rows_ready = sem("rows_ready")
        count_psum = sem("count_psum")
        tails_known = sem("tails_known")
        blocks_known = sem("blocks_known")
        tails_done = sem("tails_done")
        dm_done = sem("dm_done")
        e2_done = sem("e2_done")
        h_psum = sem("h_psum")
        h_sbuf = sem("h_sbuf")
        y_psum = sem("y_psum")
        acc_done = sem("acc_done")
        ld_blk = [sem(f"ld_blk{u}") for u in range(U)]
        xg_psum = sem("xg_psum")
        xgT_done = sem("xgT_done")
        w1_ready = sem("w1_ready")
        hT_psum = sem("hT_psum")
        hT_done = sem("hT_done")
        yb_psum = sem("yb_psum")
        yb_ready = sem("yb_ready")
        yb_sent = [sem(f"yb_sent{u}") for u in range(U)]
        ld_y = [[sem(f"ld_y{k}_{q}") for q in range(QUADS)] for k in range(2)]
        gates_known = sem("gates_known")
        weighed = sem("weighed")
        low_added = sem("low_added")
        pool_added = [sem(f"pool_added{q}") for q in range(QUADS)]
        last_done = sem("last_done")
        out_done = sem("out_done")
        stored = sem("stored")
        dve_step = sem("dve_step")
        pool_step = sem("pool_step")

        def all_turns(eng, body, peeled=1):
            for turn in range(peeled):
                for u in range(U):
                    body(turn * U + u, turn, u)
            with eng.Fori(peeled, TURNS - 1) as turn:
                for u in range(U):
                    body(turn * U + u, turn, u)
            for u in range(U):
                body((TURNS - 1) * U + u, TURNS - 1, u)

        beside = [(q, i) for q in range(QUADS) for i in range((q + 1) * QT - BESIDE[q], (q + 1) * QT)]

        def refine(E, link, dst, v, y):
            for step in range(3):
                link(E.tensor_tensor(y, v, dst, ALU.mult))
                if E is nc.vector:
                    link(E.scalar_tensor_tensor(y, y, -0.5, dst, ALU.mult, ALU.mult))
                    last = E.scalar_tensor_tensor(dst, y, 1.5, dst, ALU.add, ALU.mult)
                else:
                    link(E.tensor_tensor(y, y, dst, ALU.mult))
                    link(E.tensor_scalar(y, y, -0.5, 1.5, ALU.mult, ALU.add))
                    last = E.tensor_tensor(dst, y, dst, ALU.mult)
                if step < 2:
                    link(last)
            return last

        block = ctx.enter_context(nc.Block())

        @block.sync
        def _(sp):
            sp.dma_start(w_sb[:], w_small).then_inc(ld_w, 16)
            cols = [slice(q * QW, (q + 1) * QW) for q in range(QUADS)]
            tiles = [slice(q * QT, (q + 1) * QT) for q in range(QUADS)]
            for g in range(GROUPS):
                quads = range(g * QG, (g + 1) * QG)
                for q in quads:
                    sp.dma_start(xT_sb[:, cols[q]], x_cols[:, cols[q]]).then_inc(ld_xT[q], 16)
                    sp.dma_start(x_sb[:, tiles[q], :], x_rows[:, tiles[q], :]).then_inc(ld_x[q], 16)
                for q in quads:
                    sp.dma_start(cT_sb[:, cols[q]], ctx_cols[:, cols[q]]).then_inc(ld_cT[q], 16)
            sp.dma_start(w1_sb[:, NE, :], w1_cols[:, NE, :]).then_inc(ld_shared, 16)
            sp.dma_start(w2_sb[:, NE, :, :], w2_cols[:, NE, :, :]).then_inc(ld_shared, 16)
            sp.wait_ge(route_consts, 1)
            for k in range(SPARE):
                r = NE * REGION + k * P
                sp.dma_start(routed[r:r + P, :], empty_row[:]).then_inc(tails_done, 16)
            sp.dma_start(w1_sb[:, 0:NE, :], w1_cols[:, 0:NE, :]).then_inc(ld_experts, 16)
            sp.dma_start(w2_sb[:, 0:NE, :, :], w2_cols[:, 0:NE, :, :]).then_inc(ld_experts, 16)
            sp.wait_ge(tails_known, 1)
            for e in range(NE):
                r = sp.value_load(tail_row[0:1, e:e + 1], min_val=0, max_val=NE * REGION - P)
                sp.dma_start(routed[bass.ds(r, P), :], empty_row[:]).then_inc(tails_done, 16)
            sp.wait_ge(blocks_known, 1)

            def look_up(b):
                r = sp.value_load(block_row[0:1, bass.ds(b, 1)], min_val=0, max_val=(NE * REGION + (SPARE - 1) * P))
                if isinstance(b, int) and b < EARLY:
                    return r, sp.value_load(high_needed[0:1, b:b + 1], min_val=1, max_val=2)
                return r, None

            ahead = [look_up(b) for b in range(2)]
            sp.wait_ge(tails_done, 16 * (SPARE + NE))
            sp.wait_ge(sent_low, 16 * TILES)

            def load_block(b, turn, u):
                first = isinstance(turn, int) and turn == 0
                r, high = ahead[b] if first and u < 2 else look_up(b)
                if high is not None:
                    sp.wait_ge(rows_ready, high)
                elif isinstance(b, int) and b == EARLY:
                    sp.wait_ge(rows_ready, 2)
                if not first:
                    sp.wait_ge(w1_ready, b - U + 1)
                sp.dma_start(xg[:, u, :], routed[bass.ds(r, P), :]).then_inc(ld_blk[u], 16)

            all_turns(sp, load_block, peeled=EARLY // U + 1)
            low = sp.value_load(low_done[0:1, 0:1], min_val=U + 1, max_val=BLOCKS + U)
            sp.wait_ge(yb_ready, low)
            for q in range(QUADS):
                sp.dma_start(y_in[0][:, q * QT:(q + 1) * QT, :],
                             picked[q * QW:(q + 1) * QW, :].rearrange("(i p) d -> p i d", p=P)).then_inc(ld_y[0][q], 16)
            for u in range(U):
                sp.wait_ge(yb_sent[u], 16 * TURNS)
            for q in range(QUADS):
                sp.dma_start(y_in[1][:, tiles[q], :],
                             picked[T + q * QW:T + (q + 1) * QW, :].rearrange("(i p) d -> p i d", p=P)
                             ).then_inc(ld_y[1][q], 16)
            for q in range(QUADS - 1):
                sp.wait_ge(out_done, q + 1)
                sp.wait_ge(pool_added[q], BESIDE[q])
                sp.dma_start(out_rows[:, tiles[q], :], acc[:, tiles[q], :]).then_inc(stored, 16)
            for half in range(2):
                at = (QUADS - 1) * QT + half * QT // 2
                sp.wait_ge(last_done, half + 1)
                sp.dma_start(out_rows[:, at:at + QT // 2, :], acc[:, at:at + QT // 2, :]).then_inc(stored, 16)
            sp.wait_ge(stored, 16 * (QUADS + 1))

        @block.gpsimd
        def _(pool):
            steps = [0]

            def link(ins):
                steps[0] += 1
                ins.then_inc(pool_step, 1)
                pool.wait_ge(pool_step, steps[0])

            G = nc.gpsimd
            link(G.memset(ident[:], 0.0))
            G.affine_select(out=ident[:], in_=ident[:], compare_op=ALU.not_equal, fill=1.0, base=0,
                            pattern=[[-1, P]], channel_multiplier=1).then_inc(ident_done, 1)
            pool.wait_ge(ident_done, 1)
            link(G.memset(ident_b[:], 0.0))
            link(G.affine_select(out=ident_b[:], in_=ident_b[:], compare_op=ALU.not_equal, fill=1.0, base=0,
                                 pattern=[[-1, P]], channel_multiplier=1))
            link(G.memset(centre[:], -1.0 / D))
            link(G.affine_select(out=centre[:], in_=centre[:], compare_op=ALU.not_equal, fill=1.0 - 1.0 / D, base=0,
                                 pattern=[[-1, P]], channel_multiplier=1))
            link(G.memset(causal[:], 0.0))
            for b in range(2):
                rows = slice(b * S, (b + 1) * S)
                link(G.affine_select(out=causal[rows, :], in_=causal[rows, :], compare_op=ALU.is_ge,
                                     fill=MASKED, base=0, pattern=[[-1, S]], channel_multiplier=1))
            G.memset(probs[:], 0.0).then_inc(consts_done, 1)
            pool.wait_ge(consts_done, 1)
            link(G.iota(rank_key[:], pattern=[[0, GT], [-1, NE]], base=NE, channel_multiplier=0,
                        allow_small_or_imprecise_dtypes=True))
            link(G.iota(region_start[:], pattern=[[0, GT], [REGION, NE]], base=0, channel_multiplier=0,
                        allow_small_or_imprecise_dtypes=True))
            link(G.iota(block_no[:], pattern=[[1, BLOCKS]], base=0, channel_multiplier=0,
                        allow_small_or_imprecise_dtypes=True))
            link(G.memset(ones8[:], 1.0))
            link(G.memset(ones_b[:], 1.0))
            link(G.affine_select(out=before[:], in_=ones_b[:], compare_op=ALU.is_gt, fill=0.0, base=0,
                                 pattern=[[1, P]], channel_multiplier=-1))
            link(G.memset(empty_row[:], 0.0))
            link(G.iota(empty_row[:, D:D + 1].bitcast(I32), pattern=[[0, 1]], base=NOWHERE, channel_multiplier=0))
            link(G.memset(sent[:, :, :, D + 1:ROW], 0.0))
            G.iota(sent[:, :, :, D].bitcast(I32), pattern=[[P, TILES], [T, 2]], base=0,
                   channel_multiplier=1).then_inc(route_consts, 1)
            G.memset(mark_only[:], 0.0).then_inc(rows_ready, 1)
            pool.wait_ge(rows_ready, 1)
            pool.wait_ge(route_consts, 1)
            tiles = slice(0, GT)
            pool.wait_ge(guess1_done, 1)
            refine(G, link, rstd1[:, tiles], ve[:, tiles], newton[:, tiles]).then_inc(norm1_known, 1)
            pool.wait_ge(norm1_known, 1)
            for g in range(GROUPS):
                pool.wait_ge(exp_done, g + 1)
                half = S
                link(G.tensor_tensor(part[:], probs[:, g, :, 0:S], probs[:, g, :, S:P], ALU.add))
                while half > 2:
                    half //= 2
                    link(G.tensor_tensor(part[:, :, 0:half], part[:, :, 0:half], part[:, :, half:2 * half], ALU.add))
                G.tensor_tensor(sums[:, g, :], part[:, :, 0], part[:, :, 1], ALU.add).then_inc(sums_known, 1)
                pool.wait_ge(sums_known, g + 1)
            pool.wait_ge(guess2_done, 1)
            link(refine(G, link, rstd2[:, tiles], ve[:, tiles], newton[:, tiles]))
            link(G.tensor_tensor(shift2[:, tiles], mv2[:, tiles, 0], rstd2[:, tiles], ALU.mult))
            G.tensor_scalar(shift2[:, tiles], shift2[:, tiles], -1.0, None, ALU.mult).then_inc(norm2_known[0], 1)
            for g in range(GROUPS):
                pool.wait_ge(placed, g + 1)
                for k in range(2):
                    if k:
                        pool.wait_ge(copied, g + 1)
                    for i in range(g * GT, (g + 1) * GT):
                        if not k:
                            pool.wait_ge(x2n_done, i + 1)
                        G.indirect_dma_start(routed, bass.IndirectOffsetOnAxis(place[:, i, k:k + 1].bitcast(U32), 0),
                                             sent[:, i, k, :], None).then_inc(sent_high if k else sent_low, 16)

            pool.wait_ge(sent_high, 16 * TILES)
            G.memset(mark_only[:], 0.0).then_inc(rows_ready, 1)
            pool.wait_ge(rows_ready, 2)
            for b in range(BLOCKS):
                u = b % U
                pool.wait_ge(yb_ready, b + 1)
                G.indirect_dma_start(picked, bass.IndirectOffsetOnAxis(goes_to[:, b:b + 1], 0), y_sb[:, u, :], None,
                                     bounds_check=2 * T - 1, oob_is_err=False).then_inc(yb_sent[u], 16)
            for u in range(U):
                pool.wait_ge(yb_sent[u], 16 * TURNS)
            G.memset(mark_only[:], 1.0).then_inc(yb_ready, U)
            pool.wait_ge(low_added, 1)
            for n, (q, i) in enumerate(beside):
                pool.wait_ge(weighed, n + 1)
                G.tensor_tensor(acc[:, i, :], acc[:, i, :], y_in[1][:, i, :], ALU.add).then_inc(pool_added[q], 1)

        @block.tensor
        def _(pe):
            mm = nc.tensor.matmul

            def keep_busy(n):
                for _ in range(n):
                    mm(ps_count[:, 0:P], ident[:], ident[:], start=True, stop=True)

            pe.wait_ge(ident_done, 1)
            keep_busy(6)
            pe.wait_ge(wq_centred, 1)
            mm(ps_o[0][:, 0:D], wq_c[:], wk_sb, start=True, stop=True).then_inc(qkw_psum, 1)

            def project_t(q):
                pe.wait_ge(ld_xT[q], 16)
                if q == 0:
                    pe.wait_ge(qkw_done, 1)
                if q >= 2:
                    pe.wait_ge(t_sbuf, q - 1)
                mm(ps_t[q % 2][:], qk_w[:], xT_sb[:, q * QW:(q + 1) * QW], start=True, stop=True).then_inc(t_psum, 1)

            def project_v(q):
                pe.wait_ge(ld_cT[q], 16)
                if q == 1:
                    pe.wait_ge(s_read, 1)
                elif q == 2:
                    pe.wait_ge(t_sbuf, QUADS)
                elif q == 3:
                    pe.wait_ge(x2T_done, QG)
                for i in range(QT):
                    at = q * QW + i * P
                    last = mm(ps_v[q][:, i * D:(i + 1) * D], cT_sb[:, at:at + P], wv_sb, start=True, stop=True)
                last.then_inc(v_psum, 1)

            def score(g):
                pe.wait_ge(t_sbuf, QG * (g + 1))
                for q in range(QG * g, QG * (g + 1)):
                    pe.wait_ge(ld_cT[q], 16)
                mm(ps_s[g][:], ident_b[:], causal[:].unsqueeze(1).to_broadcast([P, GT, S]), start=True, stop=False)
                for i in range(GT):
                    for b in range(2):
                        at = (g * GT + i) * P + b * S
                        last = mm(ps_s[g][b * S:(b + 1) * S, i * S:(i + 1) * S], tT[:, at:at + S],
                                  cT_sb[:, at:at + S], start=False, stop=(i == GT - 1))
                last.then_inc(s_psum, 1)

            def transpose_probs(g):
                pe.wait_ge(exp_done, g + 1)
                if g:
                    pe.wait_ge(pT_done, QG * g)
                for q in range(QG):
                    for i in range(QT):
                        last = nc.tensor.transpose(ps_pT[q][:, i * P:(i + 1) * P], probs[:, g, q * QT + i, :], ident[:])
                    last.then_inc(pT_psum, 1)

            def attend(g):
                if g == 0:
                    pe.wait_ge(t_sbuf, QUADS)
                    pe.wait_ge(gw_done, 1)
                for q in range(QG):
                    pe.wait_ge(pT_done, QG * g + q + 1)
                    pe.wait_ge(v_sbuf, QG * g + q + 1)
                    if g:
                        pe.wait_ge(x2_done, QG * (g - 1) + q + 1)
                    for i in range(q * QT, (q + 1) * QT):
                        last = mm(ps_o[q][:, (i % QT) * D:(i % QT + 1) * D], pT[:, i, :], v_sb[:, g * GT + i, :],
                                  start=True, stop=True)
                    last.then_inc(o_psum, 1)

            def transpose_x2(g):
                if g:
                    pe.wait_ge(x2nT_done, QG * g)
                else:
                    pe.wait_ge(v_sbuf, 2)
                for q in range(QG):
                    pe.wait_ge(x2_done, QG * g + q + 1)
                    for i in range(QT):
                        last = nc.tensor.transpose(ps_x2T[g][q][:, i * P:(i + 1) * P], x2[:, g * GT + q * QT + i, :],
                                                   ident[:])
                    last.then_inc(x2T_psum, 1)

            def transpose_x2n(g, q):
                if q == 0 and g:
                    pe.wait_ge(x2T_done, QG * (g + 1))
                elif q == 0:
                    pe.wait_ge(pT_done, QUADS)
                pe.wait_ge(x2n_done, g * GT + (q + 1) * QT)
                for i in range(QT):
                    last = nc.tensor.transpose(ps_x2nT[q][:, i * P:(i + 1) * P],
                                               sent[:, g * GT + q * QT + i, 0, 0:D], ident[:])
                last.then_inc(x2nT_psum, 1)

            def gate(g):
                if g:
                    pe.wait_ge(rank_read, g)
                else:
                    pe.wait_ge(s_read, GROUPS)
                for i in range(GT):
                    if i % QT == 0:
                        pe.wait_ge(x2T_done, QG * g + i // QT + 1)
                    last = mm(ps_route[:, i * NE:(i + 1) * NE], x2T[:, i * P:(i + 1) * P], gw_c[:],
                              start=True, stop=True)
                last.then_inc(l_psum, 1)

            def rank(g):
                pe.wait_ge(chosen_done, g + 1)
                at = GT * NE
                mm(ps_route[:, at:at + GT * NE], before[:], chosen[:, g * GT:(g + 1) * GT, :], start=True, stop=False)
                for t in range((g + 1) * GT - 1):
                    i = max(t + 1 - g * GT, 0)
                    last = mm(ps_route[:, at + i * NE:at + GT * NE], ones_b[:],
                              chosen[:, t:t + 1, :].to_broadcast([P, GT - i, NE]), start=False,
                              stop=(t == (g + 1) * GT - 2))
                last.then_inc(rank_psum, 1)

            def count():
                for t in range(TILES):
                    last = mm(ps_count[:, 0:NE], ones_b[:], chosen[:, t, :], start=(t == 0), stop=(t == TILES - 1))
                last.then_inc(count_psum, 1)

            def up(q, c0, c1):
                if q == 0 and c0 == 0:
                    pe.wait_ge(ld_shared, 32)
                    pe.wait_ge(x2T_done, QG)
                if c0 == 0:
                    pe.wait_ge(x2nT_done, q + 1)
                for c in range(c0, c1):
                    n = q * HC + c
                    if n >= 2:
                        pe.wait_ge(h_sbuf, n - 1)
                    mm(ps_up[n % 2][:], w1_sb[:, NE, c * P:(c + 1) * P], x2nT[:, q * QW:(q + 1) * QW],
                       start=True, stop=True).then_inc(h_psum, 1)

            def down(q):
                pe.wait_ge(h_sbuf, HC * (q + 1))
                if q >= 2:
                    pe.wait_ge(acc_done, q - 1)
                elif q == 0:
                    pe.wait_ge(x2_done, QUADS)
                for i in range(QT):
                    for c in range(HC):
                        last = mm(ps_y[q % 2][:, i * D:(i + 1) * D], h_sb[:, q % 2, c, i * P:(i + 1) * P],
                                  w2_sb[:, NE, c, :], start=(c == 0), stop=(c == HC - 1))
                last.then_inc(y_psum, 1)

            keep_busy(1)
            project_t(0)
            project_t(1)
            pe.wait_ge(consts_done, 1)
            mm(ps_o[0][:, 0:NE], centre[:], gw_sb, start=True, stop=True).then_inc(gw_psum, 1)
            score(0)
            project_t(2)
            project_t(3)
            project_v(0)
            score(1)
            transpose_probs(0)
            project_v(1)
            attend(0)
            transpose_probs(1)
            transpose_x2(0)
            gate(0)
            project_v(2)
            project_v(3)
            attend(1)
            rank(0)
            keep_busy(8)
            transpose_x2n(0, 0)
            keep_busy(3)
            up(0, 0, 2)
            transpose_x2n(0, 1)
            up(0, 2, HC)
            transpose_x2(1)
            up(1, 0, 2)
            gate(1)
            down(0)
            rank(1)
            count()
            up(1, 2, HC)
            transpose_x2n(1, 0)
            transpose_x2n(1, 1)
            for q in range(2, QUADS - 1):
                up(q, 0, 2)
                down(q - 1)
                up(q, 2, HC)
            down(QUADS - 2)

            def turn_rows(b, turn, u):
                pe.wait_ge(ld_blk[u], 16 * (turn + 1))
                if not (isinstance(b, int) and b == 0):
                    pe.wait_ge(xgT_done, b)
                nc.tensor.transpose(ps_xg[:, 0:P], xg[:, u, 0:D], ident[:]).then_inc(xg_psum, 1)

            def block_up(b, u):
                pe.wait_ge(w1_ready, b + 1)
                for c in range(HC):
                    last = mm(ps_hT[u][:, c * P:(c + 1) * P], w1_blk[:, u, c * P:(c + 1) * P], xgT[:, u, :],
                              start=True, stop=True)
                last.then_inc(hT_psum, 1)

            def block_down(b, turn, u):
                e = pe.value_load(block_expert[0:1, bass.ds(b, 1)], min_val=0, max_val=NE)
                pe.wait_ge(hT_done, b + 1)
                if isinstance(b, int) and b == 0:
                    pe.wait_ge(acc_done, QUADS - 1)
                if not (isinstance(turn, int) and turn == 0):
                    pe.wait_ge(yb_ready, b - U + 1)
                for c in range(HC):
                    last = mm(ps_yb[u][:, 0:D], hT[:, u, c * P:(c + 1) * P],
                              w2_sb[:, bass.ds(e, 1), c, :].rearrange("p a d -> p (a d)"),
                              start=(c == 0), stop=(c == HC - 1))
                last.then_inc(yb_psum, 1)

            pe.wait_ge(blocks_known, 1)
            pe.wait_ge(ld_experts, 32)
            pe.wait_ge(acc_done, QUADS - 2)
            turn_rows(0, 0, 0)
            turn_rows(1, 0, 1)
            block_up(0, 0)

            def block(b, turn, u):
                last_turn = isinstance(b, int)
                if not last_turn or b + 2 < BLOCKS:
                    turn_rows(b + 2, turn + (u + 2) // U, (u + 2) % U)
                if not last_turn or b + 1 < BLOCKS:
                    block_up(b + 1, (u + 1) % U)
                block_down(b, turn, u)

            all_turns(pe, block)
            up(QUADS - 1, 0, HC)
            pe.wait_ge(yb_ready, BLOCKS)
            down(QUADS - 1)

        @block.scalar
        def _(act):
            A = nc.scalar.activation
            act.wait_ge(qkw_psum, 1)
            A(qk_w[:], ps_o[0][:, 0:D], ACT.Copy, scale=SCALE).then_inc(qkw_done, 1)

            def evacuate_t(q):
                act.wait_ge(t_psum, q + 1)
                A(tT[:, q * QW:(q + 1) * QW], ps_t[q % 2][:], ACT.Copy).then_inc(t_sbuf, 1)

            def evacuate_v(q):
                act.wait_ge(v_psum, q + 1)
                A(v_sb[:, q * QT:(q + 1) * QT, :], ps_v[q][:].rearrange("p (i d) -> p i d", i=QT),
                  ACT.Copy).then_inc(v_sbuf, 1)

            def softmax_exp(g):
                act.wait_ge(s_ready, g + 1)
                for b in range(2):
                    rows = slice(b * S, (b + 1) * S)
                    last = A(probs[rows, g, :, b * S:(b + 1) * S], s_sb[rows, g, :, :], ACT.Exp)
                last.then_inc(exp_done, 1)

            def evacuate_pT(g):
                for q in range(QG):
                    act.wait_ge(pT_psum, QG * g + q + 1)
                    if g and q == 0:
                        act.wait_ge(o_psum, QG * g)
                    A(pT[:, q * QT:(q + 1) * QT, :], ps_pT[q][:].rearrange("p (i q) -> p i q", i=QT),
                      ACT.Copy).then_inc(pT_done, 1)

            def evacuate_x2T(g):
                for q in range(QG):
                    act.wait_ge(x2T_psum, QG * g + q + 1)
                    if g and q == 0:
                        act.wait_ge(l_psum, g)
                    A(x2T[:, q * QW:(q + 1) * QW], ps_x2T[g][q][:], ACT.Copy).then_inc(x2T_done, 1)

            def normalise(g, q):
                act.wait_ge(norm2_known[g], 1)
                for i in range(g * GT + q * QT, g * GT + (q + 1) * QT):
                    A(sent[:, i, 0, 0:D], x2[:, i, :], ACT.Identity, bias=shift2[:, i:i + 1],
                      scale=rstd2[:, i:i + 1]).then_inc(x2n_done, 1)

            def evacuate_x2nT(g, q):
                n = QG * g + q
                act.wait_ge(x2nT_psum, n + 1)
                A(x2nT[:, n * QW:(n + 1) * QW], ps_x2nT[q][:], ACT.Copy).then_inc(x2nT_done, 1)

            def hidden(q, c0, c1):
                for c in range(c0, c1):
                    act.wait_ge(h_psum, HC * q + c + 1)
                    if q >= 2 and c == 0:
                        act.wait_ge(y_psum, q - 1)
                    A(h_sb[:, q % 2, c, :], ps_up[(q * HC + c) % 2][:], ACT.Silu).then_inc(h_sbuf, 1)

            evacuate_t(0)
            evacuate_t(1)
            act.wait_ge(gw_psum, 1)
            A(gw_c[:], ps_o[0][:, 0:NE], ACT.Copy).then_inc(gw_done, 1)
            evacuate_t(2)
            evacuate_t(3)
            act.wait_ge(consts_done, 1)
            softmax_exp(0)
            evacuate_v(0)
            evacuate_pT(0)
            evacuate_v(1)
            softmax_exp(1)
            evacuate_x2T(0)
            evacuate_pT(1)
            evacuate_v(2)
            evacuate_v(3)
            A(table_loaded[:], ident[0:1, 0:1], ACT.Silu)
            act.wait_ge(route_consts, 1)
            normalise(0, 0)
            evacuate_x2nT(0, 0)
            normalise(0, 1)
            hidden(0, 0, 2)
            evacuate_x2nT(0, 1)
            hidden(0, 2, HC)
            evacuate_x2T(1)
            normalise(1, 0)
            normalise(1, 1)
            hidden(1, 0, HC)
            evacuate_x2nT(1, 0)
            evacuate_x2nT(1, 1)
            hidden(2, 0, 2)
            act.wait_ge(dm_done, GROUPS)
            A(e2[:], dm2[:], ACT.Exp).then_inc(e2_done, 1)
            hidden(2, 2, HC)

            def block_hidden(b, turn, u):
                act.wait_ge(hT_psum, b + 1)
                A(hT[:, u, :], ps_hT[u][:], ACT.Silu).then_inc(hT_done, 1)

            all_turns(act, block_hidden)
            hidden(QUADS - 1, 0, HC)
            act.wait_ge(gates_known, 1)
            for q, i in beside:
                act.wait_ge(ld_y[1][q], 16)
                A(y_in[1][:, i, :], y_in[1][:, i, :], ACT.Copy, scale=gates[:, i, 1:2]).then_inc(weighed, 1)

        @block.vector
        def _(dve):
            steps = [0]

            def link(ins):
                steps[0] += 1
                ins.then_inc(dve_step, 1)
                dve.wait_ge(dve_step, steps[0])

            V = nc.vector

            def guess(dst, var, v):
                link(V.tensor_scalar(v, var, EPS, None, ALU.add))
                link(V.tensor_scalar(dst.bitcast(I32), v.bitcast(I32), 1, None, ALU.logical_shift_right))
                return V.tensor_scalar(dst.bitcast(I32), dst.bitcast(I32), -1.0, RSQRT_MAGIC, ALU.mult, ALU.add)

            def rsqrt(dst, var, y, v):
                link(guess(dst, var, v))
                link(refine(V, link, dst, v, y))

            def statistics(src, mv, tiles):
                for i in tiles:
                    last = V.bn_stats(stat[:, i, :], src[:, i, :])
                link(last)
                for i in tiles:
                    last = V.bn_aggr(mv[:, i, :], stat[:, i, :])
                link(last)

            def statistics1(q):
                dve.wait_ge(ld_x[q], 16)
                statistics(x_sb, mv1, range(q * QT, (q + 1) * QT))

            def norm1(g):
                tiles = slice(g * GT, (g + 1) * GT)
                if g == 0:
                    guess(rstd1[:, tiles], mv1[:, tiles, 1], ve[:, tiles]).then_inc(guess1_done, 1)
                else:
                    rsqrt(rstd1[:, tiles], mv1[:, tiles, 1], newton[:, tiles], ve[:, tiles])

            def softmax(g):
                dve.wait_ge(s_psum, g + 1)
                scores = ps_s[g][:].rearrange("p (i s) -> p i s", s=S)
                link(V.reduce_max(s_max[:], scores, AX_X))
                V.tensor_tensor(s_sb[:, g, :, :], scores, s_max[:].unsqueeze(2).to_broadcast([P, GT, S]),
                                ALU.subtract).then_inc(s_read, 1)
                dve.wait_ge(s_read, g + 1)
                if g == 0:
                    dve.wait_ge(norm1_known, 1)
                V.tensor_tensor(s_sb[:, g, :, :], s_sb[:, g, :, :],
                                rstd1[:, g * GT:(g + 1) * GT].unsqueeze(2).to_broadcast([P, GT, S]),
                                ALU.mult).then_inc(s_ready, 1)

            def residual(g):
                dve.wait_ge(sums_known, g + 1)
                link(V.reciprocal(rsum[:], sums[:, g, :]))
                for q in range(QG):
                    dve.wait_ge(o_psum, QG * g + q + 1)
                    for i in range(q * QT, (q + 1) * QT):
                        last = V.scalar_tensor_tensor(x2[:, g * GT + i, :], ps_o[q][:, (i % QT) * D:(i % QT + 1) * D],
                                                      rsum[:, i:i + 1], x_sb[:, g * GT + i, :], ALU.mult, ALU.add)
                    last.then_inc(x2_done, 1)

            def statistics2(g):
                dve.wait_ge(x2_done, QG * (g + 1))
                statistics(x2, mv2, range(g * GT, (g + 1) * GT))

            def norm2(g):
                tiles = slice(g * GT, (g + 1) * GT)
                if g == 0:
                    guess(rstd2[:, tiles], mv2[:, tiles, 1], ve[:, tiles]).then_inc(guess2_done, 1)
                    return
                rsqrt(rstd2[:, tiles], mv2[:, tiles, 1], newton[:, tiles], ve[:, tiles])
                V.scalar_tensor_tensor(shift2[:, tiles], mv2[:, tiles, 0], -1.0, rstd2[:, tiles], ALU.mult,
                                       ALU.mult).then_inc(norm2_known[g], 1)

            def wide(a):
                return a.unsqueeze(2).to_broadcast([P, GT, NE])

            def mark(one_hot, values, top, key):
                link(V.tensor_tensor(tmp[:], values, wide(top), ALU.is_equal))
                link(V.tensor_tensor(tmp[:], tmp[:], rank_key[:], ALU.mult))
                link(V.reduce_max(key, tmp[:], AX_X))
                link(V.tensor_tensor(one_hot, tmp[:], wide(key), ALU.is_equal))

            def choose(g):
                tiles = slice(g * GT, (g + 1) * GT)
                dve.wait_ge(l_psum, g + 1)
                logits = ps_route[:, 0:GT * NE].rearrange("p (i e) -> p i e", e=NE)
                link(V.reduce_max(m1[:], logits, AX_X))
                mark(first[:], logits, m1[:], key1[:])
                link(V.scalar_tensor_tensor(rest[:], first[:], TAKEN, logits, ALU.mult, ALU.add))
                link(V.reduce_max(m2[:], rest[:], AX_X))
                mark(second[:], rest[:], m2[:], key2[:])
                V.tensor_tensor(chosen[:, tiles, :], first[:], second[:], ALU.add).then_inc(chosen_done, 1)
                V.tensor_tensor(dm[:, tiles], m2[:], m1[:], ALU.subtract)
                link(V.tensor_tensor(best_is_low[:, tiles], key1[:], key2[:], ALU.is_gt))

            def gate_exponents(g):
                tiles = slice(g * GT, (g + 1) * GT)
                link(V.tensor_tensor(dm[:, tiles], dm[:, tiles], rstd2[:, tiles], ALU.mult))
                link(V.tensor_tensor(dm2[:, tiles, 1], dm[:, tiles], best_is_low[:, tiles], ALU.mult))
                V.tensor_tensor(dm2[:, tiles, 0], dm[:, tiles], dm2[:, tiles, 1], ALU.subtract).then_inc(dm_done, 1)

            def assign(g):
                dve.wait_ge(rank_psum, g + 1)
                ranks = ps_route[:, GT * NE:2 * GT * NE].rearrange("p (i e) -> p i e", e=NE)
                V.tensor_tensor(rest[:], ranks, region_start[:], ALU.add).then_inc(rank_read, 1)
                dve.wait_ge(rank_read, g + 1)
                tiles = slice(g * GT, (g + 1) * GT)
                link(V.tensor_tensor(tmp[:], chosen[:, tiles, :], rest[:], ALU.mult))
                V.reduce_max(place_high[:], tmp[:], AX_X)
                link(V.reduce_sum(place_sum[:], tmp[:], AX_X))
                V.tensor_copy(place[:, tiles, 1], place_high[:])
                V.tensor_tensor(place[:, tiles, 0], place_sum[:], place_high[:], ALU.subtract).then_inc(placed, 1)

            def weigh():
                dve.wait_ge(e2_done, 1)
                link(V.tensor_tensor(e_sum[:], e2[:, :, 0], e2[:, :, 1], ALU.add))
                link(V.reciprocal(e_sum[:], e_sum[:]))
                V.tensor_tensor(gates[:], e2[:], e_sum[:].unsqueeze(2).to_broadcast([P, TILES, 2]),
                                ALU.mult).then_inc(gates_known, 1)
                dve.wait_ge(gates_known, 1)

            def add_results(k, q, to):
                dve.wait_ge(ld_y[k][q], 16)
                for i in range(q * QT, (q + 1) * QT - k * BESIDE[q]):
                    last = V.scalar_tensor_tensor(acc[:, i, :], y_in[k][:, i, :], gates[:, i, k:k + 1], to[:, i, :],
                                                  ALU.mult, ALU.add)
                return last

            def copy_rows(g):
                tiles = slice(g * GT, (g + 1) * GT)
                dve.wait_ge(x2n_done, GT * (g + 1))
                V.tensor_copy(sent[:, tiles, 1, 0:D], sent[:, tiles, 0, 0:D]).then_inc(copied, 1)

            def plan_blocks():
                dve.wait_ge(count_psum, 1)
                counts = ps_count[0:1, 0:NE]
                V.tensor_tensor(tail_row[:], counts, region_start[0:1, 0, :], ALU.add).then_inc(tails_known, 1)
                link(V.tensor_scalar(count_i[:], counts, float(P - 1), None, ALU.add))
                dve.wait_ge(norm2_known[0], 1)
                gate_exponents(0)
                gate_exponents(1)
                link(V.tensor_scalar(nblk_i[:], count_i[:], P.bit_length() - 1, None, ALU.logical_shift_right))
                link(V.tensor_copy(nblk[:], nblk_i[:]))
                link(V.tensor_tensor_scan(cum[:], ones8[:], nblk[:], 0.0, ALU.mult, ALU.add))
                link(V.tensor_scalar(low_done[:], cum[:, NE - 2:NE - 1], float(U), None, ALU.add))
                link(V.tensor_scalar(skip[:], nblk[:], -float(P), float(REGION), ALU.mult, ALU.add))
                link(V.tensor_tensor(passed[:], block_no[:].unsqueeze(2).to_broadcast([1, BLOCKS, NE]),
                                     cum[:].unsqueeze(1).to_broadcast([1, BLOCKS, NE]), ALU.is_ge))
                link(V.reduce_sum(of_f[:], passed[:], AX_X))
                link(V.tensor_tensor(passed2[:], passed[:], skip[:].unsqueeze(1).to_broadcast([1, BLOCKS, NE]), ALU.mult))
                link(V.reduce_sum(row_f[:], passed2[:], AX_X))
                link(V.tensor_scalar(high_needed[:], of_f[:], 1.0, 1.0, ALU.min, ALU.add))
                link(V.tensor_copy(block_expert[:], of_f[:]))
                V.scalar_tensor_tensor(block_row[:], block_no[:], float(P), row_f[:], ALU.mult,
                                       ALU.add).then_inc(blocks_known, 1)

            def add_shared(q):
                dve.wait_ge(y_psum, q + 1)
                tiles = slice(q * QT, (q + 1) * QT)
                V.tensor_tensor(acc[:, tiles, :], ps_y[q % 2][:].rearrange("p (i d) -> p i d", i=QT), x2[:, tiles, :],
                                ALU.add).then_inc(acc_done, 1)

            dve.wait_ge(ld_w, 16)
            statistics(wq_sb.unsqueeze(1), mv1, range(1))
            V.tensor_scalar(wq_c[:], wq_sb, mv1[:, 0, 0:1], None, ALU.subtract).then_inc(wq_centred, 1)
            dve.wait_ge(wq_centred, 1)
            statistics1(0)
            statistics1(1)
            norm1(0)
            statistics1(2)
            softmax(0)
            statistics1(3)
            norm1(1)
            softmax(1)
            residual(0)
            statistics2(0)
            norm2(0)
            dve.wait_ge(route_consts, 1)
            choose(0)
            assign(0)
            residual(1)
            copy_rows(0)
            statistics2(1)
            norm2(1)
            choose(1)
            assign(1)
            plan_blocks()
            copy_rows(1)
            add_shared(0)
            add_shared(1)
            weigh()
            dve.wait_ge(blocks_known, 1)
            dve.wait_ge(ld_experts, 32)

            def expert_of(b):
                return V.value_load(block_expert[0:1, bass.ds(b, 1)], min_val=0, max_val=NE)

            def stage(b, u, e):
                dve.wait_ge(xg_psum, b + 1)
                V.tensor_copy(xgT[:, u, :], ps_xg[:, 0:P]).then_inc(xgT_done, 1)
                V.tensor_copy(w1_blk[:, u, :], w1_sb[:, bass.ds(e, 1), :].rearrange("p a h -> p (a h)"))
                V.tensor_copy(goes_to[:, bass.ds(b, 1)], xg[:, u, D:D + 1].bitcast(U32)).then_inc(w1_ready, 1)

            def result(b, turn, u):
                dve.wait_ge(yb_psum, b + 1)
                if not (isinstance(turn, int) and turn == 0):
                    dve.wait_ge(yb_sent[u], 16 * turn)
                V.tensor_copy(y_sb[:, u, :], ps_yb[u][:, 0:D]).then_inc(yb_ready, 1)

            stage(0, 0, expert_of(0))
            stage(1, 1, expert_of(1))
            add_shared(2)

            def block(b, turn, u):
                more = not isinstance(b, int) or b + 2 < BLOCKS
                if more:
                    e = expert_of(b + 2)
                if not isinstance(b, int) or b > 0:
                    result(b - 1, turn if u else turn - 1, (u - 1) % U)
                if more:
                    stage(b + 2, (u + 2) % U, e)

            all_turns(dve, block, peeled=2)
            result(BLOCKS - 1, TURNS - 1, U - 1)
            for q in range(QUADS - 1):
                add_results(0, q, acc)
            add_results(0, QUADS - 1, x2).then_inc(low_added, 1)
            dve.wait_ge(low_added, 1)
            for q in range(QUADS - 1):
                add_results(1, q, acc).then_inc(out_done, 1)
            link(add_results(1, QUADS - 1, acc))
            dve.wait_ge(pool_added[QUADS - 1], BESIDE[QUADS - 1])
            dve.wait_ge(y_psum, QUADS)
            for half in range(2):
                at = half * QT // 2
                tiles = slice((QUADS - 1) * QT + at, (QUADS - 1) * QT + at + QT // 2)
                y = ps_y[(QUADS - 1) % 2][:, at * D:(at + QT // 2) * D].rearrange("p (i d) -> p i d", d=D)
                V.tensor_tensor(acc[:, tiles, :], y, acc[:, tiles, :], ALU.add).then_inc(last_done, 1)


def kernel(x, ctx_1024, L0_xattn_w_q, L0_xattn_w_k, L0_xattn_w_v, L0_ffn_shared_w1, L0_ffn_shared_w2,
           L0_ffn_experts_w1, L0_ffn_experts_w2, L0_ffn_gate_w):
    import numpy as np
    import concourse.bacc as bacc
    from concourse.bass_utils import run_bass_kernel_spmd

    B, S, D = x.shape
    tiles = B * S // P
    HID = L0_ffn_shared_w1.shape[0]
    NE = L0_ffn_gate_w.shape[0]
    w1 = np.concatenate([np.asarray(L0_ffn_experts_w1), np.asarray(L0_ffn_shared_w1)[None]])
    w2 = np.concatenate([np.asarray(L0_ffn_experts_w2), np.asarray(L0_ffn_shared_w2)[None]])
    laid_out = {
        "x_rows": np.asarray(x).reshape(tiles, P, D).transpose(1, 0, 2),
        "x_cols": np.asarray(x).reshape(B * S, D).T,
        "ctx_cols": np.asarray(ctx_1024).reshape(B * S, D).T,
        "w_small": np.concatenate([np.asarray(L0_xattn_w_q).T, np.asarray(L0_xattn_w_k).T,
                                   np.asarray(L0_xattn_w_v), np.asarray(L0_ffn_gate_w).T], axis=1),
        "w1_cols": w1.transpose(2, 0, 1),
        "w2_cols": w2.transpose(2, 0, 1).reshape(HID // P, P, NE + 1, D).transpose(1, 2, 0, 3),
    }
    nc = bacc.Bacc("TRN2", target_bir_lowering=False, num_devices=1)
    arrays, args = {}, []
    for name, a in laid_out.items():
        arrays[name] = np.ascontiguousarray(a)
        args.append(nc.dram_tensor(name, a.shape, mybir.dt.from_np(a.dtype), kind="ExternalInput").ap())
    args.append(nc.dram_tensor("out_rows", (P, tiles, D), F32, kind="ExternalOutput").ap())
    spare = expert_blocks(B * S, NE) - 2 * B * S // P
    args.append(nc.dram_tensor("routed", (NE * (B * S + P) + spare * P, ROW), F32, kind="Internal").ap())
    args.append(nc.dram_tensor("picked", (2 * B * S, D), F32, kind="Internal").ap())
    build(nc, *args)
    r = run_bass_kernel_spmd(nc, [arrays], core_ids=[0])
    return np.ascontiguousarray(r.results[0]["out_rows"].transpose(1, 0, 2)).reshape(B, S, D)
```
